# Optimizing a Trainium2 kernel written in Bass

```python
import numpy as np
import jax
import jax.numpy as jnp

def _softmax(x, axis=-1):
    return jax.nn.softmax(x, axis=axis)

def _gelu(x):
    return jax.nn.gelu(x, approximate=True)

def _silu(x):
    return jax.nn.silu(x)

def _sigmoid(x):
    return jax.nn.sigmoid(x)

def _layernorm(x, axis=-1, eps=1e-05):
    m = jnp.mean(x, axis=axis, keepdims=True)
    v = jnp.var(x, axis=axis, keepdims=True)
    return (x - m) / jnp.sqrt(v + eps)

def _scatter_add(tgt, idx, src, axis=0):
    return tgt.at[idx].add(src)

def _segment_sum(src, seg, n):
    return jax.ops.segment_sum(src, seg, n)
kernel_name = 'mk_gnn_preln_d1_gnn_r8_1869bc'

def setup_inputs(seed: int=0):
    np.random.seed(seed)
    _w = jnp.asarray

    def _rec_inputs():
        import jax
        import jax.numpy as jnp
        _gk = jax.random.key(seed)
        x = -0.0001006 + 1 * jax.random.normal(jax.random.fold_in(_gk, 1), (6250, 96), jnp.float32)
        src = jax.random.randint(jax.random.fold_in(_gk, 2), (200000,), 0, 6250, jnp.int32)
        dst = jnp.minimum((6250 * jax.random.uniform(jax.random.fold_in(_gk, 3), (200000,)) ** 2.0).astype(jnp.int32), 49999)
        _o = jnp.argsort(dst, stable=True)
        src = src[_o]
        dst = dst[_o]
        edge_attr_32 = 0.000196303 + 1.00016 * jax.random.normal(jax.random.fold_in(_gk, 11), (200000, 32), jnp.float32)
        return (x, src, dst, edge_attr_32)
    x, src, dst, edge_attr_32 = _rec_inputs()

    def _L0_gnn_setup():
        import jax, jax.numpy as jnp
        import numpy as np
        N, E = (6250, 100000)
        DIN = DOUT = 96
        DE = 32

        def _egnn_conv(x, src, dst, edge_attr, W_msg, W_edge, W_root, b):
            msg = x[src] @ W_msg + edge_attr @ W_edge
            agg = jax.ops.segment_max(msg, dst, num_segments=x.shape[0])
            agg = jnp.where(jnp.isneginf(agg), 0.0, agg)
            return agg + x @ W_root + b
        key = jax.random.key(seed)
        ks = jax.random.split(key, 10)
        rn = lambda k, sh, sc: jax.random.normal(k, sh, jnp.float32) * sc
        return {'X': rn(ks[0], (N, DIN), 1.0), 'edge_index': jax.random.randint(ks[1], (2, E), 0, N, jnp.int32), 'edge_attr': rn(ks[2], (E, DE), 1.0), 'W1_msg': rn(ks[3], (DIN, DOUT), DIN ** (-0.5)), 'W1_edge': rn(ks[4], (DE, DOUT), DE ** (-0.5)), 'W1_root': rn(ks[5], (DIN, DOUT), DIN ** (-0.5)), 'b1': jnp.zeros((DOUT,), jnp.float32), 'W2_msg': rn(ks[6], (DOUT, DOUT), DOUT ** (-0.5)), 'W2_edge': rn(ks[7], (DE, DOUT), DE ** (-0.5)), 'W2_root': rn(ks[8], (DOUT, DOUT), DOUT ** (-0.5)), 'b2': jnp.zeros((DOUT,), jnp.float32)}
    _L0_gnn_all = _L0_gnn_setup()
    _L0_gnn_in = {k: v for k, v in _L0_gnn_all.items() if k in ('W1_msg', 'W1_edge', 'W1_root', 'b1', 'W2_msg', 'W2_edge', 'W2_root', 'b2')}
    del _L0_gnn_all
    return {'x': x, 'src': src, 'dst': dst, 'edge_attr_32': edge_attr_32, 'L0_gnn_W1_msg': _L0_gnn_in['W1_msg'], 'L0_gnn_W1_edge': _L0_gnn_in['W1_edge'], 'L0_gnn_W1_root': _L0_gnn_in['W1_root'], 'L0_gnn_b1': _L0_gnn_in['b1'], 'L0_gnn_W2_msg': _L0_gnn_in['W2_msg'], 'L0_gnn_W2_edge': _L0_gnn_in['W2_edge'], 'L0_gnn_W2_root': _L0_gnn_in['W2_root'], 'L0_gnn_b2': _L0_gnn_in['b2']}

def reference(x, src, dst, edge_attr_32, L0_gnn_W1_msg, L0_gnn_W1_edge, L0_gnn_W1_root, L0_gnn_b1, L0_gnn_W2_msg, L0_gnn_W2_edge, L0_gnn_W2_root, L0_gnn_b2):
    import jax
    import jax.numpy as jnp

    def _L0_gnn_ref(X, edge_index, edge_attr, W1_msg, W1_edge, W1_root, b1, W2_msg, W2_edge, W2_root, b2):
        import jax, jax.numpy as jnp
        import numpy as np
        N, E = (6250, 100000)
        DIN = DOUT = 96
        DE = 32

        def _egnn_conv(x, src, dst, edge_attr, W_msg, W_edge, W_root, b):
            msg = x[src] @ W_msg + edge_attr @ W_edge
            agg = jax.ops.segment_max(msg, dst, num_segments=x.shape[0])
            agg = jnp.where(jnp.isneginf(agg), 0.0, agg)
            return agg + x @ W_root + b
        src, dst = (edge_index[0], edge_index[1])
        c1 = jax.nn.leaky_relu(_egnn_conv(X, src, dst, edge_attr, W1_msg, W1_edge, W1_root, b1))
        c2 = jax.nn.leaky_relu(_egnn_conv(c1, src, dst, edge_attr, W2_msg, W2_edge, W2_root, b2))
        return c2
    edge_index = jnp.stack([src, dst])
    h = jnp.maximum(_layernorm(x, axis=-1), 0.0)
    x = x + _L0_gnn_ref(h, edge_index, edge_attr_32, L0_gnn_W1_msg, L0_gnn_W1_edge, L0_gnn_W1_root, L0_gnn_b1, L0_gnn_W2_msg, L0_gnn_W2_edge, L0_gnn_W2_root, L0_gnn_b2)
    return x

_drawn_inputs = setup_inputs


def setup_inputs(seed=0):
    import zlib

    import numpy as np

    out = dict(_drawn_inputs(seed))
    spreads = {'L0_gnn_b1': (0.0, 0.295), 'L0_gnn_b2': (0.0, 0.429)}
    factors = {}
    for name, (base, spread) in spreads.items():
        noise = np.random.default_rng([zlib.crc32(name.encode()), seed]).standard_normal(out[name].shape)
        drawn = base * np.exp(spread * noise) if base else spread * noise
        out[name] = jnp.asarray(drawn.astype(out[name].dtype))
    for name, factor in factors.items():
        out[name] = (out[name] * factor).astype(out[name].dtype)
    return out
```

```python
import concourse.bass as bass
from concourse import mybir
from contextlib import ExitStack

P = 128
N_NODES, N_EDGES, D, DE = 6250, 200000, 96, 32

NODE_CHUNK = 5
NODE_CHUNKS = 10
NODE_TILES = NODE_CHUNK * NODE_CHUNKS
NODE_ROWS = P * NODE_TILES

GROUP = 4
CHUNK_GROUPS = 7
CHUNK = GROUP * CHUNK_GROUPS
CHUNKS = 56
STEPS = CHUNK * CHUNKS
EDGE_ROWS = P * STEPS
ROUNDS = CHUNKS // 2
GROUPS = STEPS // GROUP

SEARCH = 448
SEARCH_COLS = NODE_TILES + 1
SEARCH_BATCH = 17
META = 2 * CHUNK + 1
assert SEARCH * SEARCH == EDGE_ROWS and SEARCH_COLS % SEARCH_BATCH == 0

BIG = 3.4e38
EPS = 1e-5
SLOPE = 0.01


def build(nc, x, meta, ea_t, dst_runs, prev_last, dst_rows, row_last, w_nodes, w_edges, biases, out):
    fp32, i32 = mybir.dt.float32, mybir.dt.int32
    ALU, ACT, AX = mybir.AluOpType, mybir.ActivationFunctionType, mybir.AxisListType

    y_table = nc.dram_tensor("y_table", (NODE_ROWS, D), fp32, kind="Internal").ap()
    maxima = nc.dram_tensor("maxima", (EDGE_ROWS + 1, D), fp32, kind="Internal").ap()
    maxima_runs = maxima[0:EDGE_ROWS, :].rearrange("(p t) d -> p (t d)", p=P)
    y_runs = y_table.rearrange("(p k) d -> p (k d)", p=P)

    with ExitStack() as ctx:
        def sb(name, shape, dt=fp32):
            return ctx.enter_context(nc.sbuf_tensor(name, shape, dt))

        def sem(name):
            return ctx.enter_context(nc.semaphore(name))

        x_sb = sb("x_sb", [P, NODE_TILES * D])
        root_sb = sb("root_sb", [P, NODE_TILES * D])
        ring = sb("ring", [P, 2 * CHUNK * D])
        squares = ring[:, 0:NODE_TILES * D]
        ea = sb("ea", [P, 2, CHUNK_GROUPS * P])
        meta_sb = sb("meta_sb", [P, 2, META], i32)
        same = sb("same", [P, 2, CHUNK])
        cut = sb("cut", [P, 2, CHUNK])
        dst_sb = sb("dst_sb", [P, STEPS], i32)
        prev_sb = sb("prev_sb", [P, 1], i32)
        rows_sb = sb("rows_sb", [P, SEARCH_COLS, SEARCH], i32)
        row_last_sb = sb("row_last_sb", [P, SEARCH], i32)
        junk_act = sb("junk_act", [P, 2, SEARCH], mybir.dt.bfloat16)
        junk_dve = sb("junk_dve", [P, STEPS], mybir.dt.bfloat16)
        node_id_i = sb("node_id_i", [P, SEARCH_COLS], i32)
        node_id = sb("node_id", [P, SEARCH_COLS])
        node_mid = sb("node_mid", [P, SEARCH_COLS])
        signs = sb("signs", [P, SEARCH_COLS])
        row_f = sb("row_f", [P, SEARCH_COLS])
        row_i = sb("row_i", [P, SEARCH_COLS], i32)
        in_row = sb("in_row", [P, SEARCH_COLS])
        ends = sb("ends", [P, SEARCH_COLS])
        has_edges = sb("has_edges", [P, NODE_TILES])
        agg_row_f = sb("agg_row_f", [P, NODE_TILES])
        agg_row = sb("agg_row", [P, NODE_TILES], i32)
        agg_idx = sb("agg_idx", [P, 2, NODE_CHUNK], i32)
        agg = sb("agg", [P, 2, NODE_CHUNK * D])
        h = sb("h", [P, 2, NODE_CHUNK * D])
        hT = sb("hT", [D, 2, NODE_CHUNK * P])
        y_sb = sb("y_sb", [P, 2, NODE_CHUNK * D])
        pre = sb("pre", [P, 2, NODE_CHUNK * D])
        res = sb("res", [P, 2, NODE_CHUNK * D])
        stats = sb("stats", [P, 4, NODE_TILES])
        ident = sb("ident", [P, P])
        w_node_sb = sb("w_node_sb", [D, 2, 2 * D])
        w_edge_sb = sb("w_edge_sb", [P, 2, GROUP * D])
        bias_sb = sb("bias_sb", [P, 2, D])
        zero_row = sb("zero_row", [1, D])
        zero_state = sb("zero_state", [P, D])
        run_base_i = sb("run_base_i", [P, 1], i32)
        run_base = sb("run_base", [P, 1])
        dst_first = sb("dst_first", [P, 1])
        first_len = sb("first_len", [P, 1])
        goes_on = sb("goes_on", [P, 1])
        carry_cut = sb("carry_cut", [P, 1])
        one_segment = sb("one_segment", [P, 1])
        through = sb("through", [P, 1])
        through_cut = sb("through_cut", [P, D])
        through_cutT = sb("through_cutT", [D, P])
        patch_row_f = sb("patch_row_f", [P, 1])
        patch_row = sb("patch_row", [P, 1], i32)
        carryT = sb("carryT", [D, P + 1])
        patch_in = sb("patch_in", [P, D])
        patched = sb("patched", [P, D])

        psum = ctx.enter_context(nc.psum_tensor("psum", [P, 8 * 512], fp32))

        def edge_bank(g):
            return psum[:, 512 * g:512 * g + GROUP * D]

        hT_ps = psum[0:D, 0:NODE_CHUNK * P]

        def node_ps(half, term):
            bank = 2 + 2 * half + term
            return psum[:, 512 * bank:512 * bank + NODE_CHUNK * D]

        lastT_ps = psum[0:D, 3584:3584 + P]
        carry_ps = psum[:, 3584 + P:3584 + P + D]

        x_in = sem("x_in")
        ident_zeroed = sem("ident_zeroed")
        ident_ready = sem("ident_ready")
        blocks_zeroed = sem("blocks_zeroed")
        w_in = sem("w_in")
        zero_ready = sem("zero_ready")
        zero_stored = sem("zero_stored")
        search_in = sem("search_in")
        dst_in = sem("dst_in")
        pool_chain = sem("pool_chain")
        mids_ready = sem("mids_ready")
        signs_ready = sem("signs_ready")
        rows_found = sem("rows_found")
        rows_in = [sem(f"rows_in{b}") for b in range(SEARCH_COLS // SEARCH_BATCH)]
        dve_chain = sem("dve_chain")
        centred = sem("centred")
        squared = sem("squared")
        var_ready = sem("var_ready")
        std_ready = sem("std_ready")
        agg_rows_ready = sem("agg_rows_ready")
        through_ready = sem("through_ready")
        throughT_ready = sem("throughT_ready")
        throughT_copied = sem("throughT_copied")
        patch_row_ready = sem("patch_row_ready")
        h_ready = sem("h_ready")
        hT_ready = sem("hT_ready")
        hT_copied = sem("hT_copied")
        node_ready = sem("node_ready")
        y_copied = sem("y_copied")
        y_stored = [sem("y_stored0"), sem("y_stored1")]
        root_stored = sem("root_stored")
        meta_in = [sem("meta_in0"), sem("meta_in1")]
        ea_in = [sem("ea_in0"), sem("ea_in1")]
        gathered = [sem(f"gathered{s}") for s in range(2 * CHUNK_GROUPS)]
        edge_ready = sem("edge_ready")
        same_ready = sem("same_ready")
        cut_ready = sem("cut_ready")
        msg_ready = sem("msg_ready")
        steps_done = sem("steps_done")
        maxima_stored = [sem("maxima_stored0"), sem("maxima_stored1")]
        lastT_ready = sem("lastT_ready")
        carryT_ready = sem("carryT_ready")
        carry_ready = sem("carry_ready")
        patch_in_ready = sem("patch_in_ready")
        patched_ready = sem("patched_ready")
        patch_stored = sem("patch_stored")
        idx_ready = sem("idx_ready")
        agg_in = [sem("agg_in0"), sem("agg_in1")]
        pre_ready = sem("pre_ready")
        act_ready = sem("act_ready")
        res_ready = sem("res_ready")
        out_stored = [sem("out_stored0"), sem("out_stored1")]

        block = ctx.enter_context(nc.Block())

        def rounds(eng, layer, body):
            if layer == 0:
                body(0, 0)
                with eng.Fori(1, ROUNDS) as i:
                    body(i, i)
            else:
                with eng.Fori(0, ROUNDS) as i:
                    body(i, i + ROUNDS)

        def node_rounds(eng, stage, body):
            n = NODE_CHUNKS // 2
            if stage == 0:
                body(0, 0)
                with eng.Fori(1, n) as i:
                    body(i, i)
            else:
                with eng.Fori(0, n) as i:
                    body(i, i + n * stage)

        def past(n):
            return not (isinstance(n, int) and n < 1)

        def ring_chunk(half):
            return ring[:, half * CHUNK * D:(half + 1) * CHUNK * D]

        def ring_group(slot):
            return ring[:, slot * GROUP * D:(slot + 1) * GROUP * D]

        def ring_step(slot, j):
            at = (slot * GROUP + j) * D
            return ring[:, at:at + D]

        @block.sync
        def _(sp):
            sp.dma_start(row_last_sb[:, :], row_last.to_broadcast((P, SEARCH))).then_inc(search_in, 16)
            sp.dma_start(x_sb[:, :], x.rearrange("(p k) d -> p (k d)", p=P)).then_inc(x_in, 16)
            for layer in range(2):
                sp.dma_start(w_node_sb[:, layer, :], w_nodes[layer]).then_inc(w_in, 16)
                sp.dma_start(bias_sb[:, layer, :], biases[layer].to_broadcast((P, D))).then_inc(w_in, 16)
            sp.wait_ge(blocks_zeroed, 1)
            for layer in range(2):
                for j in range(GROUP):
                    sp.dma_start(w_edge_sb[j * DE:(j + 1) * DE, layer, j * D:(j + 1) * D],
                                 w_edges[layer]).then_inc(w_in, 16)
            sp.dma_start(dst_sb[:, :], dst_runs).then_inc(dst_in, 16)
            sp.dma_start(prev_sb[:, :], prev_last).then_inc(dst_in, 16)
            sp.wait_ge(zero_ready, 1)
            sp.dma_start(maxima[EDGE_ROWS:EDGE_ROWS + 1, :], zero_row[:, :]).then_inc(zero_stored, 16)

            def load_round(i, m):
                for half in range(2):
                    if past(m):
                        sp.wait_ge(steps_done, GROUP * CHUNK_GROUPS * (2 * m + half - 1))
                    sp.dma_start(meta_sb[:, half, :], meta[bass.ds(2 * i + half, 1), :, :]
                                 .rearrange("a p c -> (a p) c")).then_inc(meta_in[half], 16)
                    if past(m):
                        sp.wait_ge(edge_ready, CHUNK_GROUPS * (2 * m + half - 1))
                    sp.dma_start(ea[:, half, :], ea_t[bass.ds(2 * i + half, 1), :, :]
                                 .rearrange("a p c -> (a p) c")).then_inc(ea_in[half], 16)

            rounds(sp, 0, load_round)
            rounds(sp, 1, load_round)

            out_runs = out.rearrange("(p k) d -> p (k d)", p=P)

            def store_round(i, m):
                for half in range(2):
                    sp.wait_ge(res_ready, 2 * i + half + 1)
                    sp.dma_start(out_runs[:, bass.ds((2 * i + half) * (NODE_CHUNK * D), NODE_CHUNK * D)],
                                 res[:, half, :]).then_inc(out_stored[half], 16)

            node_rounds(sp, 2, store_round)
            for half in range(2):
                sp.wait_ge(out_stored[half], 16 * (NODE_CHUNKS // 2))

        @block.gpsimd
        def _(pool):
            links = [0]

            def link(ins):
                links[0] += 1
                ins.then_inc(pool_chain, 1)
                pool.wait_ge(pool_chain, links[0])

            link(pool.iota(node_id_i[:, :], pattern=[[1, SEARCH_COLS]], base=-1, channel_multiplier=NODE_TILES))
            link(pool.tensor_copy(node_id[:, :], node_id_i[:, :]))
            pool.tensor_scalar(node_mid[:, :], node_id[:, :], 0.5, None, ALU.add).then_inc(mids_ready, 1)
            link(pool.iota(run_base_i[:, :], pattern=[[0, 1]], base=0, channel_multiplier=STEPS))
            pool.tensor_copy(run_base[:, :], run_base_i[:, :]).then_inc(mids_ready, 1)
            pool.memset(w_edge_sb[:, :, :], 0.0).then_inc(blocks_zeroed, 1)
            pool.memset(zero_row[:, :], 0.0).then_inc(zero_ready, 1)
            pool.memset(ident[:, :], 0.0).then_inc(ident_zeroed, 1)
            pool.wait_ge(ident_zeroed, 1)
            pool.affine_select(out=ident[:, :], in_=ident[:, :], compare_op=ALU.not_equal, fill=1.0,
                               base=0, pattern=[[-1, P]], channel_multiplier=1).then_inc(ident_ready, 1)
            for b in range(SEARCH_COLS // SEARCH_BATCH):
                cols = slice(b * SEARCH_BATCH, (b + 1) * SEARCH_BATCH)
                pool.wait_ge(signs_ready, (b + 1) * SEARCH_BATCH)
                pool.tensor_scalar(row_f[:, cols], signs[:, cols], 0.5, SEARCH / 2,
                                   ALU.mult, ALU.add).then_inc(rows_found, 1)
                pool.wait_ge(rows_found, 2 * b + 1)
                pool.tensor_copy(row_i[:, cols], row_f[:, cols]).then_inc(rows_found, 1)
                pool.wait_ge(rows_found, 2 * b + 2)
                for k in range(b * SEARCH_BATCH, (b + 1) * SEARCH_BATCH):
                    pool.indirect_dma_start(
                        out=rows_sb[:, k, :], out_offset=None, in_=dst_rows[:, :],
                        in_offset=bass.IndirectOffsetOnAxis(ap=row_i[:, k:k + 1], axis=0),
                    ).then_inc(rows_in[b], 16)

            def gather_edges(layer):
                for half in range(2):
                    pool.wait_ge(y_stored[half], 16 * (NODE_CHUNKS // 2) * (layer + 1))

                def gather_round(i, m):
                    for half in range(2):
                        pool.wait_ge(meta_in[half], 16 * (m + 1))
                        if past(m):
                            pool.wait_ge(maxima_stored[half], 16 * m)
                            pool.wait_ge(steps_done, GROUP * (CHUNK_GROUPS * (2 * m + half - 1) + 1))
                        pool.nop(nofuse=True)
                        for g in range(CHUNK_GROUPS):
                            slot = half * CHUNK_GROUPS + g
                            for j in range(GROUP):
                                t = g * GROUP + j
                                pool.indirect_dma_start(
                                    out=ring_step(slot, j), out_offset=None, in_=y_table[:, :],
                                    in_offset=bass.IndirectOffsetOnAxis(ap=meta_sb[:, half, t:t + 1], axis=0),
                                ).then_inc(gathered[slot], 16)

                rounds(pool, layer, gather_round)

            def patch_runs(layer):
                for half in range(2):
                    pool.wait_ge(maxima_stored[half], 16 * ROUNDS * (layer + 1))
                pool.wait_ge(patch_row_ready, 1)
                if layer:
                    pool.wait_ge(patch_stored, 16 * layer)
                pool.indirect_dma_start(
                    out=patch_in[:, :], out_offset=None, in_=maxima[:, :],
                    in_offset=bass.IndirectOffsetOnAxis(ap=patch_row[:, 0:1], axis=0),
                ).then_inc(patch_in_ready, 16)
                pool.wait_ge(patched_ready, layer + 1)
                pool.indirect_dma_start(
                    out=maxima[:, :], out_offset=bass.IndirectOffsetOnAxis(ap=patch_row[:, 0:1], axis=0),
                    in_=patched[:, :], in_offset=None,
                ).then_inc(patch_stored, 16)
                pool.wait_ge(patch_stored, 16 * (layer + 1))

            def gather_aggregates(layer):
                pool.wait_ge(agg_rows_ready, 1)
                pool.wait_ge(zero_stored, 16)

                def agg_round(i, m):
                    n = m - NODE_CHUNKS // 2
                    for half in range(2):
                        wait_free(n, half)
                        pool.tensor_copy(agg_idx[:, half, :],
                                         agg_row[:, bass.ds((2 * i + half) * NODE_CHUNK, NODE_CHUNK)]
                                         ).then_inc(idx_ready, 1)
                        pool.wait_ge(idx_ready, 2 * n + half + 1)
                        pool.nop(nofuse=True)
                        for k in range(NODE_CHUNK):
                            pool.indirect_dma_start(
                                out=agg[:, half, k * D:(k + 1) * D], out_offset=None, in_=maxima[:, :],
                                in_offset=bass.IndirectOffsetOnAxis(ap=agg_idx[:, half, k:k + 1], axis=0),
                            ).then_inc(agg_in[half], 16)

                def wait_free(n, half):
                    if past(n):
                        pool.wait_ge(pre_ready, 2 * n + half - 1)

                r = NODE_CHUNKS // 2
                if layer == 0:
                    agg_round(0, r)
                    with pool.Fori(1, r) as i:
                        agg_round(i, i + r)
                else:
                    with pool.Fori(0, r) as i:
                        agg_round(i, i + 2 * r)

            for layer in range(2):
                gather_edges(layer)
                patch_runs(layer)
                gather_aggregates(layer)

        @block.scalar
        def _(act):
            act.wait_ge(search_in, 16)
            act.wait_ge(mids_ready, 1)
            for k in range(SEARCH_COLS):
                if k >= 2:
                    act.wait_ge(signs_ready, k - 1)
                nc.scalar.activation(junk_act[:, k % 2, :], row_last_sb[:, :], ACT.Sign, scale=-1.0,
                                     bias=node_mid[:, k:k + 1], accum_out=signs[:, k:k + 1]).then_inc(signs_ready, 1)
                if k == SEARCH_BATCH:
                    act.wait_ge(centred, 1)
                    nc.scalar.activation(squares, root_sb[:, :], ACT.Square).then_inc(squared, 1)
            act.wait_ge(var_ready, 1)
            nc.scalar.activation(stats[:, 2, :], stats[:, 1, :], ACT.Sqrt).then_inc(std_ready, 1)

            act.wait_ge(throughT_ready, 1)
            nc.scalar.copy(through_cutT[:, :], lastT_ps).then_inc(throughT_copied, 1)

            def node_copies(stage):
                def copy_round(i, m):
                    for half in range(2):
                        n = 2 * m + half
                        act.wait_ge(hT_ready, n + 1)
                        if past(m):
                            act.wait_ge(node_ready, n - 1)
                        nc.scalar.copy(hT[:, half, :], hT_ps).then_inc(hT_copied, 1)
                        act.wait_ge(node_ready, n + 1)
                        if past(m):
                            act.wait_ge(y_stored[half], 16 * m)
                        nc.scalar.copy(y_sb[:, half, :], node_ps(half, 0)).then_inc(y_copied, 1)
                        act.wait_ge(y_copied, n + 1)
                        act.dma_start(y_runs[:, bass.ds((2 * i + half) * (NODE_CHUNK * D), NODE_CHUNK * D)],
                                      y_sb[:, half, :]).then_inc(y_stored[half], 16)

                node_rounds(act, stage, copy_round)

            def store_maxima(layer):
                def store_round(i, m):
                    for half in range(2):
                        act.wait_ge(steps_done, CHUNK * (2 * m + half + 1))
                        act.dma_start(maxima_runs[:, bass.ds((2 * i + half) * (CHUNK * D), CHUNK * D)],
                                      ring_chunk(half)).then_inc(maxima_stored[half], 16)

                rounds(act, layer, store_round)

            for layer in range(2):
                node_copies(layer)
                store_maxima(layer)
            for half in range(2):
                act.wait_ge(maxima_stored[half], 16 * ROUNDS * 2)

        @block.vector
        def _(dve):
            links = [0]

            def link(ins):
                links[0] += 1
                ins.then_inc(dve_chain, 1)
                dve.wait_ge(dve_chain, links[0])

            def tiles(ap):
                return ap.rearrange("p (k c) -> p k c", c=D)

            def per_tile(ap, n=NODE_TILES):
                return ap.unsqueeze(2).to_broadcast((P, n, D))

            mean, var, std, rstd = (stats[:, s, :] for s in range(4))
            dve.wait_ge(x_in, 16)
            link(nc.vector.tensor_reduce(mean, tiles(x_sb[:, :]), axis=AX.X, op=ALU.add))
            link(nc.vector.tensor_scalar(mean, mean, 1.0 / D, None, ALU.mult))
            nc.vector.tensor_tensor(tiles(root_sb[:, :]), tiles(x_sb[:, :]), per_tile(mean),
                                    ALU.subtract).then_inc(centred, 1)
            dve.wait_ge(squared, 1)
            link(nc.vector.tensor_reduce(var, tiles(squares), axis=AX.X, op=ALU.add))
            nc.vector.tensor_scalar(var, var, 1.0 / D, EPS, ALU.mult, ALU.add).then_inc(var_ready, 1)
            dve.wait_ge(std_ready, 1)
            link(nc.vector.reciprocal(rstd, std))

            dve.wait_ge(dst_in, 32)
            dve.wait_ge(mids_ready, 2)
            link(nc.vector.tensor_copy(dst_first[:, :], dst_sb[:, 0:1]))
            link(nc.vector.tensor_scalar(junk_dve[:, :], dst_sb[:, :], dst_first[:, 0:1], 0.0, ALU.is_equal,
                                         ALU.add, accum_out=first_len[:, :]))
            link(nc.vector.tensor_tensor(goes_on[:, :], prev_sb[:, :], dst_first[:, :], ALU.is_equal))
            link(nc.vector.tensor_scalar(carry_cut[:, :], goes_on[:, :], -1.0, BIG, ALU.add, ALU.mult))
            link(nc.vector.tensor_scalar(one_segment[:, :], first_len[:, :], float(STEPS), None, ALU.is_equal))
            link(nc.vector.tensor_tensor(through[:, :], goes_on[:, :], one_segment[:, :], ALU.mult))
            link(nc.vector.tensor_scalar(through[:, :], through[:, :], -1.0, BIG, ALU.add, ALU.mult))
            nc.vector.tensor_copy(through_cut[:, :], through[:, 0:1].to_broadcast((P, D))).then_inc(through_ready, 1)
            link(nc.vector.scalar_tensor_tensor(patch_row_f[:, :], first_len[:, :], -1.0, run_base[:, :],
                                                ALU.add, ALU.add))
            nc.vector.tensor_copy(patch_row[:, :], patch_row_f[:, :]).then_inc(patch_row_ready, 1)
            link(nc.vector.memset(carryT[:, 0:1], 0.0))
            link(nc.vector.memset(zero_state[:, :], 0.0))

            def root_terms(stage, i, m):
                for half in range(2):
                    dve.wait_ge(node_ready, 2 * m + half + 1)
                    nc.vector.tensor_tensor(
                        tiles(root_sb[:, bass.ds((2 * i + half) * (NODE_CHUNK * D), NODE_CHUNK * D)]),
                        tiles(node_ps(half, 1)),
                        bias_sb[:, stage, :].unsqueeze(1).to_broadcast((P, NODE_CHUNK, D)),
                        ALU.add).then_inc(root_stored, 1)

            def norm_round(i, m):
                for half in range(2):
                    if past(m):
                        dve.wait_ge(hT_ready, 2 * m + half - 1)
                    nc.vector.scalar_tensor_tensor(
                        tiles(h[:, half, :]),
                        tiles(root_sb[:, bass.ds((2 * i + half) * (NODE_CHUNK * D), NODE_CHUNK * D)]), 0.0,
                        per_tile(stats[:, 3, bass.ds((2 * i + half) * NODE_CHUNK, NODE_CHUNK)], NODE_CHUNK),
                        ALU.max, ALU.mult).then_inc(h_ready, 1)
                root_terms(0, i, m)

            def find_ends():
                for k in range(SEARCH_COLS):
                    if k % SEARCH_BATCH == 0:
                        dve.wait_ge(rows_in[k // SEARCH_BATCH], 16 * SEARCH_BATCH)
                    ins = nc.vector.tensor_scalar(junk_dve[:, 0:SEARCH], rows_sb[:, k, :], node_id[:, k:k + 1],
                                                  0.0, ALU.is_le, ALU.add, accum_out=in_row[:, k:k + 1])
                    link(ins)
                link(nc.vector.scalar_tensor_tensor(ends[:, :], row_f[:, :], float(SEARCH), in_row[:, :],
                                                    ALU.mult, ALU.add))
                link(nc.vector.tensor_tensor(has_edges[:, :], ends[:, 1:], ends[:, 0:NODE_TILES], ALU.is_gt))
                link(nc.vector.scalar_tensor_tensor(agg_row_f[:, :], ends[:, 1:], -1.0 - EDGE_ROWS,
                                                    has_edges[:, :], ALU.add, ALU.mult))
                link(nc.vector.tensor_scalar(agg_row_f[:, :], agg_row_f[:, :], float(EDGE_ROWS), None, ALU.add))
                nc.vector.tensor_copy(agg_row[:, :], agg_row_f[:, :]).then_inc(agg_rows_ready, 1)

            def reduce_edges(layer):
                def edge_round(i, m):
                    for half in range(2):
                        dve.wait_ge(meta_in[half], 16 * (m + 1))
                        nc.vector.tensor_tensor(same[:, half, :], meta_sb[:, half, CHUNK:2 * CHUNK],
                                                meta_sb[:, half, CHUNK + 1:META], ALU.is_equal).then_inc(same_ready, 1)
                        dve.wait_ge(same_ready, 2 * m + half + 1)
                        nc.vector.tensor_scalar(cut[:, half, :], same[:, half, :], -1.0, BIG,
                                                ALU.add, ALU.mult).then_inc(cut_ready, 1)
                        dve.wait_ge(cut_ready, 2 * m + half + 1)
                        for g in range(CHUNK_GROUPS):
                            slot = half * CHUNK_GROUPS + g
                            n = CHUNK_GROUPS * (2 * m + half) + g
                            dve.wait_ge(gathered[slot], 16 * GROUP * (m + 1))
                            dve.wait_ge(edge_ready, n + 1)
                            nc.vector.tensor_tensor(ring_group(slot), ring_group(slot), edge_bank(g),
                                                    ALU.add).then_inc(msg_ready, 1)
                            dve.wait_ge(msg_ready, n + 1)
                            for j in range(GROUP):
                                before = slot * GROUP + j - 1
                                prev = ring_step(0, before % (2 * CHUNK))
                                if past(GROUP * n + j):
                                    dve.wait_ge(steps_done, GROUP * n + j)
                                else:
                                    prev = zero_state[:, :]
                                nc.vector.scalar_tensor_tensor(
                                    ring_step(slot, j), prev, cut[:, half, g * GROUP + j:g * GROUP + j + 1],
                                    ring_step(slot, j), ALU.add, ALU.max).then_inc(steps_done, 1)

                rounds(dve, layer, edge_round)

            def carry_runs(layer):
                dve.wait_ge(lastT_ready, layer + 1)
                dve.wait_ge(throughT_copied, 1)
                nc.vector.tensor_tensor_scan(carryT[:, 1:P + 1], through_cutT[:, :], lastT_ps, 0.0,
                                             ALU.add, ALU.max).then_inc(carryT_ready, 1)
                dve.wait_ge(carry_ready, layer + 1)
                dve.wait_ge(patch_in_ready, 16 * (layer + 1))
                nc.vector.scalar_tensor_tensor(patched[:, :], carry_ps, carry_cut[:, 0:1], patch_in[:, :],
                                               ALU.add, ALU.max).then_inc(patched_ready, 1)

            def update(stage):
                def update_round(i, m):
                    n = m - NODE_CHUNKS // 2
                    for half in range(2):
                        cols = bass.ds((2 * i + half) * (NODE_CHUNK * D), NODE_CHUNK * D)
                        c = 2 * n + half
                        dve.wait_ge(agg_in[half], 16 * NODE_CHUNK * (n + 1))
                        nc.vector.tensor_tensor(pre[:, half, :], agg[:, half, :], root_sb[:, cols],
                                                ALU.add).then_inc(pre_ready, 1)
                        dve.wait_ge(pre_ready, c + 1)
                        if stage == 1:
                            dve.wait_ge(hT_ready, 2 * m + half - 1)
                        nc.vector.scalar_tensor_tensor(
                            h[:, half, :], pre[:, half, :], SLOPE, pre[:, half, :],
                            ALU.mult, ALU.max).then_inc(h_ready if stage == 1 else act_ready, 1)
                        if stage == 2:
                            dve.wait_ge(act_ready, 2 * i + half + 1)
                            free_res(i, half)
                            nc.vector.tensor_tensor(res[:, half, :], h[:, half, :], x_sb[:, cols],
                                                    ALU.add).then_inc(res_ready, 1)
                    if stage == 1:
                        root_terms(1, i, m)

                def free_res(i, half):
                    if past(i):
                        dve.wait_ge(out_stored[half], 16 * i)

                r = NODE_CHUNKS // 2
                if stage == 2:
                    update_round(0, 2 * r)
                    with dve.Fori(1, r) as i:
                        update_round(i, i + 2 * r)
                else:
                    node_rounds(dve, stage, update_round)

            node_rounds(dve, 0, norm_round)
            find_ends()
            reduce_edges(0)
            carry_runs(0)
            update(1)
            reduce_edges(1)
            carry_runs(1)
            update(2)

        @block.tensor
        def _(pe):
            pe.wait_ge(ident_ready, 1)
            pe.wait_ge(w_in, 16 * (4 + 2 * GROUP))
            pe.wait_ge(through_ready, 1)
            nc.tensor.transpose(lastT_ps, through_cut[:, :], ident[:, :]).then_inc(throughT_ready, 1)

            def node_products(stage):
                def product_round(i, m):
                    for half in range(2):
                        n = 2 * m + half
                        pe.wait_ge(h_ready, n + 1)
                        if past(n):
                            pe.wait_ge(hT_copied, n)
                        for k in range(NODE_CHUNK):
                            last = nc.tensor.transpose(hT_ps[:, k * P:(k + 1) * P],
                                                       h[:, half, k * D:(k + 1) * D], ident[:, :])
                        last.then_inc(hT_ready, 1)
                        pe.wait_ge(hT_copied, n + 1)
                        if past(m):
                            pe.wait_ge(y_copied, n - 1)
                            pe.wait_ge(root_stored, n - 1)
                        for k in range(NODE_CHUNK):
                            for term in range(2):
                                last = nc.tensor.matmul(
                                    node_ps(half, term)[:, k * D:(k + 1) * D], hT[:, half, k * P:(k + 1) * P],
                                    w_node_sb[:, stage, term * D:(term + 1) * D], start=True, stop=True)
                        last.then_inc(node_ready, 1)

                node_rounds(pe, stage, product_round)

            def edge_products(layer):
                for_nodes = NODE_CHUNKS * (layer + 1)
                pe.wait_ge(y_copied, for_nodes)
                pe.wait_ge(root_stored, for_nodes)

                def edge_round(i, m):
                    for half in range(2):
                        pe.wait_ge(ea_in[half], 16 * (m + 1))
                        for g in range(CHUNK_GROUPS):
                            n = CHUNK_GROUPS * (2 * m + half) + g
                            if past(n - CHUNK_GROUPS + 1):
                                pe.wait_ge(msg_ready, n - CHUNK_GROUPS + 1)
                            nc.tensor.matmul(edge_bank(g), ea[:, half, g * P:(g + 1) * P],
                                             w_edge_sb[:, layer, :], start=True, stop=True).then_inc(edge_ready, 1)

                rounds(pe, layer, edge_round)

            def carry_transposes(layer):
                pe.wait_ge(steps_done, STEPS * (layer + 1))
                if layer:
                    pe.wait_ge(patched_ready, layer)
                nc.tensor.transpose(lastT_ps, ring_step(2 * CHUNK_GROUPS - 1, GROUP - 1),
                                    ident[:, :]).then_inc(lastT_ready, 1)
                pe.wait_ge(carryT_ready, layer + 1)
                nc.tensor.transpose(carry_ps, carryT[:, 0:P], ident[0:D, 0:D]).then_inc(carry_ready, 1)
                pe.wait_ge(patched_ready, layer + 1)

            for layer in range(2):
                node_products(layer)
                edge_products(layer)
                carry_transposes(layer)


def kernel(**inputs):
    import numpy as np
    import concourse.bacc as bacc
    from concourse.bass_utils import run_bass_kernel_spmd

    def get(name):
        return np.asarray(inputs[name])

    x = np.zeros((NODE_ROWS, D), np.float32)
    x[:N_NODES] = get("x")
    src = np.zeros(EDGE_ROWS, np.int32)
    src[:N_EDGES] = get("src")
    dst = np.full(EDGE_ROWS, NODE_ROWS, np.int32)
    dst[:N_EDGES] = get("dst")
    ea = np.zeros((EDGE_ROWS, DE), np.float32)
    ea[:N_EDGES] = get("edge_attr_32")

    before = np.full(EDGE_ROWS, -1, np.int32)
    before.reshape(P, STEPS)[:, 1:] = dst.reshape(P, STEPS)[:, :-1]
    prev_last = np.full((P, 1), -1, np.int32)
    prev_last[1:, 0] = dst.reshape(P, STEPS)[:-1, -1]
    by_chunk = lambda a: a.reshape(P, CHUNKS, CHUNK).transpose(1, 0, 2)
    meta = np.concatenate([by_chunk(src), by_chunk(before)[:, :, :1], by_chunk(dst)], axis=2)
    ea_t = ea.reshape(P, CHUNKS, CHUNK_GROUPS, GROUP, DE).transpose(1, 3, 4, 2, 0)
    dst_rows = dst.reshape(SEARCH, SEARCH)

    arrays = {
        "x_rows": x,
        "meta": meta,
        "ea_t": ea_t.reshape(CHUNKS, GROUP * DE, CHUNK_GROUPS * P),
        "dst_runs": dst.reshape(P, STEPS),
        "prev_last": prev_last,
        "dst_rows": dst_rows,
        "row_last": dst_rows[:, -1].reshape(1, SEARCH),
        "w_node1": np.concatenate([get("L0_gnn_W1_msg"), get("L0_gnn_W1_root")], axis=1),
        "w_node2": np.concatenate([get("L0_gnn_W2_msg"), get("L0_gnn_W2_root")], axis=1),
        "w_edge1": get("L0_gnn_W1_edge"),
        "w_edge2": get("L0_gnn_W2_edge"),
        "bias1": get("L0_gnn_b1").reshape(1, D),
        "bias2": get("L0_gnn_b2").reshape(1, D),
    }
    arrays = {name: np.ascontiguousarray(a) for name, a in arrays.items()}

    nc = bacc.Bacc("TRN2", target_bir_lowering=False, num_devices=1)
    ap = {name: nc.dram_tensor(name, a.shape, mybir.dt.from_np(a.dtype), kind="ExternalInput").ap()
          for name, a in arrays.items()}
    out = nc.dram_tensor("out", (NODE_ROWS, D), mybir.dt.float32, kind="ExternalOutput").ap()
    build(nc, ap["x_rows"], ap["meta"], ap["ea_t"], ap["dst_runs"], ap["prev_last"], ap["dst_rows"],
          ap["row_last"], [ap["w_node1"], ap["w_node2"]], [ap["w_edge1"], ap["w_edge2"]],
          [ap["bias1"], ap["bias2"]], out)
    r = run_bass_kernel_spmd(nc, [arrays], core_ids=[0])
    return r.results[0]["out"][:N_NODES]
```

```python
import concourse.bass as bass
from concourse import mybir
from contextlib import ExitStack

P = 128
N_NODES, N_EDGES, D, DE = 6250, 200000, 96, 32

NODE_CHUNK = 5
NODE_CHUNKS = 10
NODE_TILES = NODE_CHUNK * NODE_CHUNKS
NODE_ROWS = P * NODE_TILES

GROUP = 4
CHUNK_GROUPS = 7
CHUNK = GROUP * CHUNK_GROUPS
CHUNKS = 56
STEPS = CHUNK * CHUNKS
EDGE_ROWS = P * STEPS
ROUNDS = CHUNKS // 2
GROUPS = STEPS // GROUP

SEARCH = 448
SEARCH_COLS = NODE_TILES + 1
SEARCH_BATCH = 17
HOT = {1: 3, 3: 3, 5: 3}
HOTS = len(HOT)
META = 2 * CHUNK + 1
assert SEARCH * SEARCH == EDGE_ROWS and SEARCH_COLS % SEARCH_BATCH == 0

BIG = 3.4e38
EPS = 1e-5
SLOPE = 0.01


def build(nc, x, meta, hot_src, ea_t, dst_runs, prev_last, dst_rows, row_last, w_nodes, w_edges, biases, out):
    fp32, bf16, i32 = mybir.dt.float32, mybir.dt.bfloat16, mybir.dt.int32
    ALU, ACT, AX = mybir.AluOpType, mybir.ActivationFunctionType, mybir.AxisListType

    y_table = nc.dram_tensor("y_table", (NODE_ROWS, D), fp32, kind="Internal").ap()
    maxima = nc.dram_tensor("maxima", (EDGE_ROWS + 1, D), fp32, kind="Internal").ap()
    maxima_runs = maxima[0:EDGE_ROWS, :].rearrange("(p t) d -> p (t d)", p=P)
    y_runs = y_table.rearrange("(p k) d -> p (k d)", p=P)

    with ExitStack() as ctx:
        def sb(name, shape, dt=fp32):
            return ctx.enter_context(nc.sbuf_tensor(name, shape, dt))

        def sem(name):
            return ctx.enter_context(nc.semaphore(name))

        root_sb = sb("root_sb", [P, NODE_TILES * D])
        ring = sb("ring", [P, 2 * CHUNK * D])
        x_sb = ring[:, 0:NODE_TILES * D]
        squares = x_sb
        ea = sb("ea", [P, 2, CHUNK_GROUPS * P])
        meta_sb = sb("meta_sb", [P, 2, META], i32)
        same = sb("same", [P, 2, CHUNK])
        cut = sb("cut", [P, 2, CHUNK])
        y_parts = sb("y_parts", [P, 3, NODE_TILES * D], bf16)
        dst_sb = y_parts[:, 0, 0:2 * STEPS].bitcast(i32)
        dst_junk = y_parts[:, 1, 0:STEPS]
        prev_sb = sb("prev_sb", [P, 1], i32)
        search_space = sb("search_space", [P, SEARCH_COLS * SEARCH], i32)
        rows_sb = search_space[:, :].rearrange("p (k c) -> p k c", c=SEARCH)
        wide = search_space[:, 0:(HOTS + 1) * NODE_TILES * P // 2].bitcast(bf16).rearrange(
            "p (q k e) -> p q k e", k=NODE_TILES, e=P)
        tile_no = wide[:, HOTS, :, :]
        tile_row_i = sb("tile_row_i", [P, NODE_TILES], i32)
        tile_row = sb("tile_row", [P, NODE_TILES], bf16)
        hot_sb = sb("hot_sb", [P, 2, HOTS * P], i32)
        hot_tile = sb("hot_tile", [P, 2, HOTS * P], bf16)
        minus_base = sb("minus_base", [P, 1])
        rest = sb("rest", [P, 2, NODE_CHUNK * D])
        row_last_sb = sb("row_last_sb", [P, SEARCH], i32)
        junk_act = sb("junk_act", [P, 2, SEARCH], mybir.dt.bfloat16)
        junk_dve = sb("junk_dve", [P, SEARCH], bf16)
        node_id_i = sb("node_id_i", [P, SEARCH_COLS], i32)
        node_id = sb("node_id", [P, SEARCH_COLS])
        node_mid = sb("node_mid", [P, SEARCH_COLS])
        signs = sb("signs", [P, SEARCH_COLS])
        row_f = sb("row_f", [P, SEARCH_COLS])
        row_i = sb("row_i", [P, SEARCH_COLS], i32)
        in_row = sb("in_row", [P, SEARCH_COLS])
        ends = sb("ends", [P, SEARCH_COLS])
        has_edges = sb("has_edges", [P, NODE_TILES])
        agg_row_f = sb("agg_row_f", [P, NODE_TILES])
        agg_row = sb("agg_row", [P, NODE_TILES], i32)
        agg_idx = sb("agg_idx", [P, 2, NODE_CHUNK], i32)
        agg = sb("agg", [P, 2, NODE_CHUNK * D])
        h = sb("h", [P, 2, NODE_CHUNK * D])
        hT = sb("hT", [D, 2, NODE_CHUNK * P])
        y_sb = sb("y_sb", [P, 2, NODE_CHUNK * D])
        x_again = rest
        res = y_sb
        stats = sb("stats", [P, 4, NODE_TILES])
        ident = sb("ident", [P, P])
        w_node_sb = sb("w_node_sb", [D, 2, 2 * D])
        w_edge_sb = sb("w_edge_sb", [P, 2, GROUP * D])
        bias_sb = sb("bias_sb", [P, 2, D])
        zero_row = sb("zero_row", [1, D])
        zero_state = sb("zero_state", [P, D])
        run_base_i = sb("run_base_i", [P, 1], i32)
        run_base = sb("run_base", [P, 1])
        dst_first = sb("dst_first", [P, 1])
        first_len = sb("first_len", [P, 1])
        goes_on = sb("goes_on", [P, 1])
        carry_cut = sb("carry_cut", [P, 1])
        one_segment = sb("one_segment", [P, 1])
        through = sb("through", [P, 1])
        through_cut = sb("through_cut", [P, D])
        through_cutT = sb("through_cutT", [D, P])
        patch_row_f = sb("patch_row_f", [P, 1])
        patch_row = sb("patch_row", [P, 1], i32)
        carryT = sb("carryT", [D, P + 1])
        patch_in = sb("patch_in", [P, D])
        patched = sb("patched", [P, D])

        psum = ctx.enter_context(nc.psum_tensor("psum", [P, 8 * 512], fp32))

        def edge_bank(g):
            return psum[:, 512 * g:512 * g + GROUP * D]

        def hT_ps(half):
            return psum[0:D, 3072 * half:3072 * half + NODE_CHUNK * P]

        def node_ps(half, term):
            bank = 2 + 2 * half + term
            return psum[:, 512 * bank:512 * bank + NODE_CHUNK * D]

        lastT_ps = psum[0:D, 3584:3584 + P]
        carry_ps = psum[:, 3584 + P:3584 + P + D]

        x_in = sem("x_in")
        ident_zeroed = sem("ident_zeroed")
        ident_ready = sem("ident_ready")
        blocks_zeroed = sem("blocks_zeroed")
        w_in = sem("w_in")
        zero_ready = sem("zero_ready")
        zero_stored = sem("zero_stored")
        search_in = sem("search_in")
        dst_in = sem("dst_in")
        pool_chain = sem("pool_chain")
        mids_ready = sem("mids_ready")
        signs_ready = sem("signs_ready")
        rows_found = sem("rows_found")
        rows_in = [sem(f"rows_in{b}") for b in range(SEARCH_COLS // SEARCH_BATCH)]
        dve_chain = sem("dve_chain")
        centred = sem("centred")
        squared = sem("squared")
        var_ready = sem("var_ready")
        std_ready = sem("std_ready")
        agg_rows_ready = sem("agg_rows_ready")
        through_ready = sem("through_ready")
        throughT_ready = sem("throughT_ready")
        throughT_copied = sem("throughT_copied")
        patch_row_ready = sem("patch_row_ready")
        h_ready = sem("h_ready")
        hT_ready = sem("hT_ready")
        hT_copied = sem("hT_copied")
        node_ready = sem("node_ready")
        y_copied = sem("y_copied")
        y_stored = [sem("y_stored0"), sem("y_stored1")]
        root_stored = sem("root_stored")
        meta_in = [sem("meta_in0"), sem("meta_in1")]
        ea_in = [sem("ea_in0"), sem("ea_in1")]
        gathered = [sem(f"gathered{s}") for s in range(2 * CHUNK_GROUPS)]
        edge_ready = sem("edge_ready")
        same_ready = sem("same_ready")
        cut_ready = sem("cut_ready")
        msg_ready = sem("msg_ready")
        steps_done = sem("steps_done")
        maxima_stored = [sem("maxima_stored0"), sem("maxima_stored1")]
        lastT_ready = sem("lastT_ready")
        carryT_ready = sem("carryT_ready")
        carry_ready = sem("carry_ready")
        patch_in_ready = sem("patch_in_ready")
        patched_ready = sem("patched_ready")
        patch_stored = sem("patch_stored")
        idx_ready = sem("idx_ready")
        agg_in = [sem("agg_in0"), sem("agg_in1")]
        updated = sem("updated")
        x_again_in = [sem("x_again_in0"), sem("x_again_in1")]
        hot_in = [sem("hot_in0"), sem("hot_in1")]
        hot_tile_ready = sem("hot_tile_ready")
        onehot_ready = sem("onehot_ready")
        y_hi_ready = sem("y_hi_ready")
        rest_ready = sem("rest_ready")
        y_mid_ready = sem("y_mid_ready")
        y_parts_ready = sem("y_parts_ready")
        sum_ready = sem("sum_ready")
        res_ready = sem("res_ready")
        out_stored = [sem("out_stored0"), sem("out_stored1")]

        block = ctx.enter_context(nc.Block())

        def rounds(eng, layer, body):
            if layer == 0:
                body(0, 0)
                with eng.Fori(1, ROUNDS) as i:
                    body(i, i)
            else:
                with eng.Fori(0, ROUNDS) as i:
                    body(i, i + ROUNDS)

        def node_rounds(eng, stage, body):
            n = NODE_CHUNKS // 2
            if stage == 0:
                body(0, 0)
                with eng.Fori(1, n) as i:
                    body(i, i)
            else:
                with eng.Fori(0, n) as i:
                    body(i, i + n * stage)

        def past(n):
            return not (isinstance(n, int) and n < 1)

        def ring_chunk(half):
            return ring[:, half * CHUNK * D:(half + 1) * CHUNK * D]

        def ring_group(slot):
            return ring[:, slot * GROUP * D:(slot + 1) * GROUP * D]

        def ring_step(slot, j):
            at = (slot * GROUP + j) * D
            return ring[:, at:at + D]

        @block.sync
        def _(sp):
            sp.dma_start(row_last_sb[:, :], row_last.to_broadcast((P, SEARCH))).then_inc(search_in, 16)
            sp.dma_start(x_sb, x.rearrange("(p k) d -> p (k d)", p=P)).then_inc(x_in, 16)
            for layer in range(2):
                sp.dma_start(w_node_sb[:, layer, :], w_nodes[layer]).then_inc(w_in, 16)
                sp.dma_start(bias_sb[:, layer, :], biases[layer].to_broadcast((P, D))).then_inc(w_in, 16)
            sp.wait_ge(blocks_zeroed, 1)
            for layer in range(2):
                for j in range(GROUP):
                    sp.dma_start(w_edge_sb[j * DE:(j + 1) * DE, layer, j * D:(j + 1) * D],
                                 w_edges[layer]).then_inc(w_in, 16)
            sp.dma_start(dst_sb, dst_runs).then_inc(dst_in, 16)
            sp.dma_start(prev_sb[:, :], prev_last).then_inc(dst_in, 16)
            sp.wait_ge(zero_ready, 1)
            sp.dma_start(maxima[EDGE_ROWS:EDGE_ROWS + 1, :], zero_row[:, :]).then_inc(zero_stored, 16)

            def load_hot(c, half):
                sp.dma_start(hot_sb[:, half, :], hot_src[c, :, :].rearrange("a b c -> (a b) c")
                             .to_broadcast((P, HOTS * P))).then_inc(hot_in[half], 16)

            load_hot(slice(0, 1), 0)

            def load_round(i, m):
                for half in range(2):
                    if past(2 * m + half):
                        sp.wait_ge(hot_tile_ready, 2 * m + half)
                    load_hot(bass.ds(2 * i + half + 1, 1), 1 - half)
                    if past(m):
                        sp.wait_ge(steps_done, GROUP * CHUNK_GROUPS * (2 * m + half - 1))
                    sp.dma_start(meta_sb[:, half, :], meta[bass.ds(2 * i + half, 1), :, :]
                                 .rearrange("a p c -> (a p) c")).then_inc(meta_in[half], 16)
                    if past(m):
                        sp.wait_ge(edge_ready, CHUNK_GROUPS * (2 * m + half - 1))
                    sp.dma_start(ea[:, half, :], ea_t[bass.ds(2 * i + half, 1), :, :]
                                 .rearrange("a p c -> (a p) c")).then_inc(ea_in[half], 16)

            rounds(sp, 0, load_round)
            rounds(sp, 1, load_round)

            x_runs = x.rearrange("(p k) d -> p (k d)", p=P)
            out_runs = out.rearrange("(p k) d -> p (k d)", p=P)

            sp.wait_ge(y_parts_ready, 2 * NODE_CHUNKS)

            def store_round(i, m):
                for half in range(2):
                    if past(i):
                        sp.wait_ge(res_ready, 2 * i + half - 1)
                    sp.dma_start(x_again[:, half, :],
                                 x_runs[:, bass.ds((2 * i + half) * (NODE_CHUNK * D), NODE_CHUNK * D)]
                                 ).then_inc(x_again_in[half], 16)
                for half in range(2):
                    sp.wait_ge(res_ready, 2 * i + half + 1)
                    sp.dma_start(out_runs[:, bass.ds((2 * i + half) * (NODE_CHUNK * D), NODE_CHUNK * D)],
                                 res[:, half, :]).then_inc(out_stored[half], 16)

            store_round(0, 0)
            with sp.Fori(1, NODE_CHUNKS // 2) as i:
                store_round(i, i)
            for half in range(2):
                sp.wait_ge(out_stored[half], 16 * (NODE_CHUNKS // 2))

        @block.gpsimd
        def _(pool):
            links = [0]

            def link(ins):
                links[0] += 1
                ins.then_inc(pool_chain, 1)
                pool.wait_ge(pool_chain, links[0])

            link(pool.iota(node_id_i[:, :], pattern=[[1, SEARCH_COLS]], base=-1, channel_multiplier=NODE_TILES))
            link(pool.tensor_copy(node_id[:, :], node_id_i[:, :]))
            pool.tensor_scalar(node_mid[:, :], node_id[:, :], 0.5, None, ALU.add).then_inc(mids_ready, 1)
            link(pool.iota(run_base_i[:, :], pattern=[[0, 1]], base=0, channel_multiplier=STEPS))
            pool.tensor_copy(run_base[:, :], run_base_i[:, :]).then_inc(mids_ready, 1)
            pool.tensor_scalar(minus_base[:, :], node_id[:, 0:1], 1.0, -1.0, ALU.add, ALU.mult).then_inc(mids_ready, 1)
            link(pool.iota(tile_row_i[:, :], pattern=[[1, NODE_TILES]], base=0, channel_multiplier=0))
            pool.tensor_copy(tile_row[:, :], tile_row_i[:, :]).then_inc(mids_ready, 1)
            pool.memset(w_edge_sb[:, :, :], 0.0).then_inc(blocks_zeroed, 1)
            pool.memset(zero_row[:, :], 0.0).then_inc(zero_ready, 1)
            pool.memset(ident[:, :], 0.0).then_inc(ident_zeroed, 1)
            pool.wait_ge(ident_zeroed, 1)
            pool.affine_select(out=ident[:, :], in_=ident[:, :], compare_op=ALU.not_equal, fill=1.0,
                               base=0, pattern=[[-1, P]], channel_multiplier=1).then_inc(ident_ready, 1)
            for b in range(SEARCH_COLS // SEARCH_BATCH):
                cols = slice(b * SEARCH_BATCH, (b + 1) * SEARCH_BATCH)
                pool.wait_ge(signs_ready, (b + 1) * SEARCH_BATCH)
                pool.tensor_scalar(row_f[:, cols], signs[:, cols], 0.5, SEARCH / 2,
                                   ALU.mult, ALU.add).then_inc(rows_found, 1)
                pool.wait_ge(rows_found, 2 * b + 1)
                pool.tensor_copy(row_i[:, cols], row_f[:, cols]).then_inc(rows_found, 1)
                pool.wait_ge(rows_found, 2 * b + 2)
                for k in range(b * SEARCH_BATCH, (b + 1) * SEARCH_BATCH):
                    pool.indirect_dma_start(
                        out=rows_sb[:, k, :], out_offset=None, in_=dst_rows[:, :],
                        in_offset=bass.IndirectOffsetOnAxis(ap=row_i[:, k:k + 1], axis=0),
                    ).then_inc(rows_in[b], 16)

            def gather_edges(layer):
                for half in range(2):
                    pool.wait_ge(y_stored[half], 16 * (NODE_CHUNKS // 2) * (layer + 1))

                def gather_round(i, m):
                    for half in range(2):
                        pool.wait_ge(meta_in[half], 16 * (m + 1))
                        if past(m):
                            pool.wait_ge(maxima_stored[half], 16 * m)
                            pool.wait_ge(steps_done, GROUP * (CHUNK_GROUPS * (2 * m + half - 1) + 1))
                        pool.nop(nofuse=True)
                        for g in range(CHUNK_GROUPS):
                            slot = half * CHUNK_GROUPS + g
                            for j in range(GROUP):
                                if HOT.get(g) == j:
                                    continue
                                t = g * GROUP + j
                                pool.indirect_dma_start(
                                    out=ring_step(slot, j), out_offset=None, in_=y_table[:, :],
                                    in_offset=bass.IndirectOffsetOnAxis(ap=meta_sb[:, half, t:t + 1], axis=0),
                                ).then_inc(gathered[slot], 16)

                rounds(pool, layer, gather_round)

            def patch_runs(layer):
                for half in range(2):
                    pool.wait_ge(maxima_stored[half], 16 * ROUNDS * (layer + 1))
                pool.wait_ge(patch_row_ready, 1)
                if layer:
                    pool.wait_ge(patch_stored, 16 * layer)
                pool.indirect_dma_start(
                    out=patch_in[:, :], out_offset=None, in_=maxima[:, :],
                    in_offset=bass.IndirectOffsetOnAxis(ap=patch_row[:, 0:1], axis=0),
                ).then_inc(patch_in_ready, 16)
                pool.wait_ge(patched_ready, layer + 1)
                pool.indirect_dma_start(
                    out=maxima[:, :], out_offset=bass.IndirectOffsetOnAxis(ap=patch_row[:, 0:1], axis=0),
                    in_=patched[:, :], in_offset=None,
                ).then_inc(patch_stored, 16)
                pool.wait_ge(patch_stored, 16 * (layer + 1))

            def gather_aggregates(layer):
                pool.wait_ge(agg_rows_ready, 1)
                pool.wait_ge(zero_stored, 16)

                def agg_round(i, m):
                    n = m - NODE_CHUNKS // 2
                    for half in range(2):
                        wait_free(n, half)
                        pool.tensor_copy(agg_idx[:, half, :],
                                         agg_row[:, bass.ds((2 * i + half) * NODE_CHUNK, NODE_CHUNK)]
                                         ).then_inc(idx_ready, 1)
                        pool.wait_ge(idx_ready, 2 * n + half + 1)
                        pool.nop(nofuse=True)
                        for k in range(NODE_CHUNK):
                            pool.indirect_dma_start(
                                out=agg[:, half, k * D:(k + 1) * D], out_offset=None, in_=maxima[:, :],
                                in_offset=bass.IndirectOffsetOnAxis(ap=agg_idx[:, half, k:k + 1], axis=0),
                            ).then_inc(agg_in[half], 16)

                def wait_free(n, half):
                    if past(n):
                        pool.wait_ge(updated, 2 * n + half - 1)

                r = NODE_CHUNKS // 2
                if layer == 0:
                    agg_round(0, r)
                    with pool.Fori(1, r) as i:
                        agg_round(i, i + r)
                else:
                    with pool.Fori(0, r) as i:
                        agg_round(i, i + 2 * r)

            for layer in range(2):
                gather_edges(layer)
                patch_runs(layer)
                gather_aggregates(layer)

        @block.scalar
        def _(act):
            act.wait_ge(search_in, 16)
            act.wait_ge(mids_ready, 1)
            for k in range(SEARCH_COLS):
                if k >= 2:
                    act.wait_ge(signs_ready, k - 1)
                nc.scalar.activation(junk_act[:, k % 2, :], row_last_sb[:, :], ACT.Sign, scale=-1.0,
                                     bias=node_mid[:, k:k + 1], accum_out=signs[:, k:k + 1]).then_inc(signs_ready, 1)
                if k == SEARCH_BATCH:
                    act.wait_ge(centred, 1)
                    nc.scalar.activation(squares, root_sb[:, :], ACT.Square).then_inc(squared, 1)
            act.wait_ge(var_ready, 1)
            nc.scalar.activation(stats[:, 2, :], stats[:, 1, :], ACT.Sqrt).then_inc(std_ready, 1)

            act.wait_ge(throughT_ready, 1)
            nc.scalar.copy(through_cutT[:, :], lastT_ps).then_inc(throughT_copied, 1)
            act.wait_ge(mids_ready, 3)

            def place_hot(half):
                nc.scalar.activation(hot_tile[:, half, :], hot_sb[:, half, :], ACT.Identity,
                                     bias=minus_base[:, 0:1]).then_inc(hot_tile_ready, 1)

            act.wait_ge(hot_in[0], 16)
            place_hot(0)

            def node_copies(stage):
                def copy_round(i, m):
                    for half in range(2):
                        n = 2 * m + half
                        act.wait_ge(hT_ready, n + 1)
                        if past(m):
                            act.wait_ge(node_ready, n - 1)
                        nc.scalar.copy(hT[:, half, :], hT_ps(half)).then_inc(hT_copied, 1)
                    for half in range(2):
                        n = 2 * m + half
                        cols = bass.ds((2 * i + half) * (NODE_CHUNK * D), NODE_CHUNK * D)
                        act.wait_ge(node_ready, n + 1)
                        if past(m):
                            act.wait_ge(y_stored[half], 16 * m)
                            act.wait_ge(rest_ready, n - 1)
                        nc.scalar.copy(y_sb[:, half, :], node_ps(half, 0)).then_inc(y_copied, 1)
                        act.wait_ge(y_copied, n + 1)
                        act.dma_start(y_runs[:, cols], y_sb[:, half, :]).then_inc(y_stored[half], 16)
                        nc.scalar.copy(y_parts[:, 0, cols], y_sb[:, half, :]).then_inc(y_hi_ready, 1)

                node_rounds(act, stage, copy_round)

            def store_maxima(layer):
                def store_round(i, m):
                    for half in range(2):
                        act.wait_ge(hot_in[1 - half], 16 * (m + 1 + half))
                        if past(2 * m + half):
                            act.wait_ge(onehot_ready, HOTS * (2 * m + half))
                        place_hot(1 - half)
                        act.wait_ge(steps_done, CHUNK * (2 * m + half + 1))
                        act.dma_start(maxima_runs[:, bass.ds((2 * i + half) * (CHUNK * D), CHUNK * D)],
                                      ring_chunk(half)).then_inc(maxima_stored[half], 16)

                rounds(act, layer, store_round)

            for layer in range(2):
                node_copies(layer)
                store_maxima(layer)
            for half in range(2):
                act.wait_ge(maxima_stored[half], 16 * ROUNDS * 2)

        @block.vector
        def _(dve):
            links = [0]

            def link(ins):
                links[0] += 1
                ins.then_inc(dve_chain, 1)
                dve.wait_ge(dve_chain, links[0])

            def tiles(ap):
                return ap.rearrange("p (k c) -> p k c", c=D)

            def per_tile(ap, n=NODE_TILES):
                return ap.unsqueeze(2).to_broadcast((P, n, D))

            mean, var, std, rstd = (stats[:, s, :] for s in range(4))
            dve.wait_ge(x_in, 16)
            link(nc.vector.tensor_reduce(mean, tiles(x_sb), axis=AX.X, op=ALU.add))
            link(nc.vector.tensor_scalar(mean, mean, 1.0 / D, None, ALU.mult))
            nc.vector.tensor_tensor(tiles(root_sb[:, :]), tiles(x_sb), per_tile(mean),
                                    ALU.subtract).then_inc(centred, 1)
            dve.wait_ge(squared, 1)
            link(nc.vector.tensor_reduce(var, tiles(squares), axis=AX.X, op=ALU.add))
            nc.vector.tensor_scalar(var, var, 1.0 / D, EPS, ALU.mult, ALU.add).then_inc(var_ready, 1)
            dve.wait_ge(std_ready, 1)
            link(nc.vector.reciprocal(rstd, std))

            dve.wait_ge(dst_in, 32)
            dve.wait_ge(mids_ready, 4)
            link(nc.vector.tensor_copy(dst_first[:, :], dst_sb[:, 0:1]))
            link(nc.vector.tensor_scalar(dst_junk, dst_sb, dst_first[:, 0:1], 0.0, ALU.is_equal,
                                         ALU.add, accum_out=first_len[:, :]))
            link(nc.vector.tensor_tensor(goes_on[:, :], prev_sb[:, :], dst_first[:, :], ALU.is_equal))
            link(nc.vector.tensor_scalar(carry_cut[:, :], goes_on[:, :], -1.0, BIG, ALU.add, ALU.mult))
            link(nc.vector.tensor_scalar(one_segment[:, :], first_len[:, :], float(STEPS), None, ALU.is_equal))
            link(nc.vector.tensor_tensor(through[:, :], goes_on[:, :], one_segment[:, :], ALU.mult))
            link(nc.vector.tensor_scalar(through[:, :], through[:, :], -1.0, BIG, ALU.add, ALU.mult))
            nc.vector.tensor_copy(through_cut[:, :], through[:, 0:1].to_broadcast((P, D))).then_inc(through_ready, 1)
            link(nc.vector.scalar_tensor_tensor(patch_row_f[:, :], first_len[:, :], -1.0, run_base[:, :],
                                                ALU.add, ALU.add))
            nc.vector.tensor_copy(patch_row[:, :], patch_row_f[:, :]).then_inc(patch_row_ready, 1)
            link(nc.vector.memset(carryT[:, 0:1], 0.0))
            link(nc.vector.memset(zero_state[:, :], 0.0))

            def root_terms(stage, i, m):
                for half in range(2):
                    dve.wait_ge(node_ready, 2 * m + half + 1)
                    nc.vector.tensor_tensor(
                        tiles(root_sb[:, bass.ds((2 * i + half) * (NODE_CHUNK * D), NODE_CHUNK * D)]),
                        tiles(node_ps(half, 1)),
                        bias_sb[:, stage, :].unsqueeze(1).to_broadcast((P, NODE_CHUNK, D)),
                        ALU.add).then_inc(root_stored, 1)

            def split_y(i, m):
                for half in range(2):
                    n = 2 * m + half
                    cols = bass.ds((2 * i + half) * (NODE_CHUNK * D), NODE_CHUNK * D)
                    dve.wait_ge(y_hi_ready, n + 1)
                    nc.vector.tensor_tensor(rest[:, half, :], y_sb[:, half, :], y_parts[:, 0, cols],
                                            ALU.subtract).then_inc(rest_ready, 1)
                    dve.wait_ge(rest_ready, n + 1)
                    nc.vector.tensor_copy(y_parts[:, 1, cols], rest[:, half, :]).then_inc(y_mid_ready, 1)
                    dve.wait_ge(y_mid_ready, n + 1)
                    nc.vector.tensor_tensor(y_parts[:, 2, cols], rest[:, half, :], y_parts[:, 1, cols],
                                            ALU.subtract).then_inc(y_parts_ready, 1)

            def norm_round(i, m):
                for half in range(2):
                    if past(m):
                        dve.wait_ge(hT_ready, 2 * m + half - 1)
                    nc.vector.scalar_tensor_tensor(
                        tiles(h[:, half, :]),
                        tiles(root_sb[:, bass.ds((2 * i + half) * (NODE_CHUNK * D), NODE_CHUNK * D)]), 0.0,
                        per_tile(stats[:, 3, bass.ds((2 * i + half) * NODE_CHUNK, NODE_CHUNK)], NODE_CHUNK),
                        ALU.max, ALU.mult).then_inc(h_ready, 1)
                root_terms(0, i, m)
                split_y(i, m)

            def build_onehot(q, half, built):
                dve.wait_ge(hot_tile_ready, built)
                nc.vector.tensor_tensor(
                    wide[:, q, :, :],
                    hot_tile[:, half, q * P:(q + 1) * P].unsqueeze(1).to_broadcast((P, NODE_TILES, P)),
                    tile_no, ALU.is_equal).then_inc(onehot_ready, 1)

            def find_ends():
                for k in range(SEARCH_COLS):
                    if k % SEARCH_BATCH == 0:
                        dve.wait_ge(rows_in[k // SEARCH_BATCH], 16 * SEARCH_BATCH)
                    ins = nc.vector.tensor_scalar(junk_dve[:, 0:SEARCH], rows_sb[:, k, :], node_id[:, k:k + 1],
                                                  0.0, ALU.is_le, ALU.add, accum_out=in_row[:, k:k + 1])
                    link(ins)
                link(nc.vector.scalar_tensor_tensor(ends[:, :], row_f[:, :], float(SEARCH), in_row[:, :],
                                                    ALU.mult, ALU.add))
                link(nc.vector.tensor_tensor(has_edges[:, :], ends[:, 1:], ends[:, 0:NODE_TILES], ALU.is_gt))
                link(nc.vector.scalar_tensor_tensor(agg_row_f[:, :], ends[:, 1:], -1.0 - EDGE_ROWS,
                                                    has_edges[:, :], ALU.add, ALU.mult))
                link(nc.vector.tensor_scalar(agg_row_f[:, :], agg_row_f[:, :], float(EDGE_ROWS), None, ALU.add))
                nc.vector.tensor_copy(agg_row[:, :], agg_row_f[:, :]).then_inc(agg_rows_ready, 1)

            def reduce_edges(layer):
                def edge_round(i, m):
                    for half in range(2):
                        dve.wait_ge(meta_in[half], 16 * (m + 1))
                        nc.vector.tensor_tensor(same[:, half, :], meta_sb[:, half, CHUNK:2 * CHUNK],
                                                meta_sb[:, half, CHUNK + 1:META], ALU.is_equal).then_inc(same_ready, 1)
                        dve.wait_ge(same_ready, 2 * m + half + 1)
                        nc.vector.tensor_scalar(cut[:, half, :], same[:, half, :], -1.0, BIG,
                                                ALU.add, ALU.mult).then_inc(cut_ready, 1)
                        dve.wait_ge(cut_ready, 2 * m + half + 1)
                        for g in range(CHUNK_GROUPS):
                            slot = half * CHUNK_GROUPS + g
                            n = CHUNK_GROUPS * (2 * m + half) + g
                            dve.wait_ge(gathered[slot], 16 * (GROUP - (g in HOT)) * (m + 1))
                            dve.wait_ge(edge_ready, n + 1)
                            own = GROUP * D if g not in HOT else HOT[g] * D
                            nc.vector.tensor_tensor(ring_group(slot)[:, 0:own], ring_group(slot)[:, 0:own],
                                                    edge_bank(g)[:, 0:own], ALU.add).then_inc(msg_ready, 1)
                            dve.wait_ge(msg_ready, n + 1)
                            for j in range(GROUP):
                                before = slot * GROUP + j - 1
                                prev = ring_step(0, before % (2 * CHUNK))
                                if past(GROUP * n + j):
                                    dve.wait_ge(steps_done, GROUP * n + j)
                                else:
                                    prev = zero_state[:, :]
                                nc.vector.scalar_tensor_tensor(
                                    ring_step(slot, j), prev, cut[:, half, g * GROUP + j:g * GROUP + j + 1],
                                    edge_bank(g)[:, j * D:(j + 1) * D] if HOT.get(g) == j else ring_step(slot, j),
                                    ALU.add, ALU.max).then_inc(steps_done, 1)
                            if g in HOT:
                                build_onehot(list(HOT).index(g), 1 - half, 2 * m + half + 2)

                rounds(dve, layer, edge_round)

            def carry_runs(layer):
                dve.wait_ge(lastT_ready, layer + 1)
                dve.wait_ge(throughT_copied, 1)
                nc.vector.tensor_tensor_scan(carryT[:, 1:P + 1], through_cutT[:, :], lastT_ps, 0.0,
                                             ALU.add, ALU.max).then_inc(carryT_ready, 1)
                dve.wait_ge(carry_ready, layer + 1)
                dve.wait_ge(patch_in_ready, 16 * (layer + 1))
                nc.vector.scalar_tensor_tensor(patched[:, :], carry_ps, carry_cut[:, 0:1], patch_in[:, :],
                                               ALU.add, ALU.max).then_inc(patched_ready, 1)

            def update(stage):
                def update_round(i, m):
                    n = m - NODE_CHUNKS // 2
                    for half in range(2):
                        cols = bass.ds((2 * i + half) * (NODE_CHUNK * D), NODE_CHUNK * D)
                        c = 2 * n + half
                        dve.wait_ge(agg_in[half], 16 * NODE_CHUNK * (n + 1))
                        nc.vector.tensor_tensor(agg[:, half, :], agg[:, half, :], root_sb[:, cols],
                                                ALU.add).then_inc(sum_ready, 1)
                        dve.wait_ge(sum_ready, c + 1)
                        if stage == 1:
                            dve.wait_ge(hT_ready, 2 * m + half - 1)
                        nc.vector.scalar_tensor_tensor(
                            h[:, half, :], agg[:, half, :], SLOPE, agg[:, half, :],
                            ALU.mult, ALU.max).then_inc(updated, 1)
                        if stage == 2:
                            dve.wait_ge(updated, c + 1)
                            dve.wait_ge(x_again_in[half], 16 * (i + 1))
                            if past(i):
                                dve.wait_ge(out_stored[half], 16 * i)
                            nc.vector.tensor_tensor(res[:, half, :], h[:, half, :], x_again[:, half, :],
                                                    ALU.add).then_inc(res_ready, 1)
                    if stage == 1:
                        root_terms(1, i, m)
                        split_y(i, m)

                r = NODE_CHUNKS // 2
                if stage == 2:
                    update_round(0, 2 * r)
                    with dve.Fori(1, r) as i:
                        update_round(i, i + 2 * r)
                else:
                    node_rounds(dve, stage, update_round)

            node_rounds(dve, 0, norm_round)
            find_ends()
            link(nc.vector.tensor_copy(tile_no, tile_row[:, :].unsqueeze(2).to_broadcast((P, NODE_TILES, P))))
            for q in range(HOTS):
                build_onehot(q, 0, 1)
            reduce_edges(0)
            carry_runs(0)
            update(1)
            reduce_edges(1)
            carry_runs(1)
            update(2)

        @block.tensor
        def _(pe):
            pe.wait_ge(ident_ready, 1)
            pe.wait_ge(w_in, 16 * (4 + 2 * GROUP))
            pe.wait_ge(through_ready, 1)
            nc.tensor.transpose(lastT_ps, through_cut[:, :], ident[:, :]).then_inc(throughT_ready, 1)
            pe.wait_ge(throughT_copied, 1)

            def node_products(stage):
                def product_round(i, m):
                    for half in range(2):
                        n = 2 * m + half
                        if stage == 0:
                            pe.wait_ge(h_ready, n + 1)
                        else:
                            pe.wait_ge(updated, n - NODE_CHUNKS + 1)
                        if past(m):
                            pe.wait_ge(hT_copied, n - 1)
                        for k in range(NODE_CHUNK):
                            last = nc.tensor.transpose(hT_ps(half)[:, k * P:(k + 1) * P],
                                                       h[:, half, k * D:(k + 1) * D], ident[:, :])
                        last.then_inc(hT_ready, 1)
                    for half in range(2):
                        n = 2 * m + half
                        pe.wait_ge(hT_copied, n + 1)
                        if past(m):
                            pe.wait_ge(y_copied, n - 1)
                            pe.wait_ge(root_stored, n - 1)
                        for k in range(NODE_CHUNK):
                            for term in range(2):
                                last = nc.tensor.matmul(
                                    node_ps(half, term)[:, k * D:(k + 1) * D], hT[:, half, k * P:(k + 1) * P],
                                    w_node_sb[:, stage, term * D:(term + 1) * D], start=True, stop=True)
                        last.then_inc(node_ready, 1)

                node_rounds(pe, stage, product_round)

            def edge_products(layer):
                for_nodes = NODE_CHUNKS * (layer + 1)
                pe.wait_ge(y_copied, for_nodes)
                pe.wait_ge(root_stored, for_nodes)
                pe.wait_ge(y_parts_ready, for_nodes)

                def edge_round(i, m):
                    for half in range(2):
                        pe.wait_ge(ea_in[half], 16 * (m + 1))
                        for g in range(CHUNK_GROUPS):
                            n = CHUNK_GROUPS * (2 * m + half) + g
                            if past(n - CHUNK_GROUPS + 1):
                                pe.wait_ge(steps_done, GROUP * (n - CHUNK_GROUPS + 1))
                            last = nc.tensor.matmul(edge_bank(g), ea[:, half, g * P:(g + 1) * P],
                                                    w_edge_sb[:, layer, :], start=True, stop=g not in HOT)
                            if g in HOT:
                                j, q = HOT[g], list(HOT).index(g)
                                pe.wait_ge(onehot_ready, HOTS * (2 * m + half) + q + 1)
                                for k in range(NODE_TILES):
                                    for part in range(3):
                                        last = nc.tensor.matmul(
                                            edge_bank(g)[:, j * D:(j + 1) * D], wide[:, q, k, :],
                                            y_parts[:, part, k * D:(k + 1) * D],
                                            start=False, stop=(k, part) == (NODE_TILES - 1, 2))
                            last.then_inc(edge_ready, 1)

                rounds(pe, layer, edge_round)

            def carry_transposes(layer):
                pe.wait_ge(steps_done, STEPS * (layer + 1))
                if layer:
                    pe.wait_ge(patched_ready, layer)
                nc.tensor.transpose(lastT_ps, ring_step(2 * CHUNK_GROUPS - 1, GROUP - 1),
                                    ident[:, :]).then_inc(lastT_ready, 1)
                pe.wait_ge(carryT_ready, layer + 1)
                nc.tensor.transpose(carry_ps, carryT[:, 0:P], ident[0:D, 0:D]).then_inc(carry_ready, 1)
                pe.wait_ge(patched_ready, layer + 1)

            for layer in range(2):
                node_products(layer)
                edge_products(layer)
                carry_transposes(layer)


def kernel(**inputs):
    import numpy as np
    import concourse.bacc as bacc
    from concourse.bass_utils import run_bass_kernel_spmd

    def get(name):
        return np.asarray(inputs[name])

    x = np.zeros((NODE_ROWS, D), np.float32)
    x[:N_NODES] = get("x")
    src = np.zeros(EDGE_ROWS, np.int32)
    src[:N_EDGES] = get("src")
    dst = np.full(EDGE_ROWS, NODE_ROWS, np.int32)
    dst[:N_EDGES] = get("dst")
    ea = np.zeros((EDGE_ROWS, DE), np.float32)
    ea[:N_EDGES] = get("edge_attr_32")

    before = np.full(EDGE_ROWS, -1, np.int32)
    before.reshape(P, STEPS)[:, 1:] = dst.reshape(P, STEPS)[:, :-1]
    prev_last = np.full((P, 1), -1, np.int32)
    prev_last[1:, 0] = dst.reshape(P, STEPS)[:-1, -1]
    by_chunk = lambda a: a.reshape(P, CHUNKS, CHUNK).transpose(1, 0, 2)
    meta = np.concatenate([by_chunk(src), by_chunk(before)[:, :, :1], by_chunk(dst)], axis=2)
    ea_t = ea.reshape(P, CHUNKS, CHUNK_GROUPS, GROUP, DE).transpose(1, 3, 4, 2, 0)
    dst_rows = dst.reshape(SEARCH, SEARCH)
    hot_steps = [GROUP * g + j for g, j in HOT.items()]
    hot_src = src.reshape(P, CHUNKS, CHUNK)[:, :, hot_steps].transpose(1, 2, 0).reshape(CHUNKS, 1, HOTS * P)
    hot_src = np.concatenate([hot_src, hot_src[:1]])

    arrays = {
        "x_rows": x,
        "meta": meta,
        "hot_src": hot_src,
        "ea_t": ea_t.reshape(CHUNKS, GROUP * DE, CHUNK_GROUPS * P),
        "dst_runs": dst.reshape(P, STEPS),
        "prev_last": prev_last,
        "dst_rows": dst_rows,
        "row_last": dst_rows[:, -1].reshape(1, SEARCH),
        "w_node1": np.concatenate([get("L0_gnn_W1_msg"), get("L0_gnn_W1_root")], axis=1),
        "w_node2": np.concatenate([get("L0_gnn_W2_msg"), get("L0_gnn_W2_root")], axis=1),
        "w_edge1": get("L0_gnn_W1_edge"),
        "w_edge2": get("L0_gnn_W2_edge"),
        "bias1": get("L0_gnn_b1").reshape(1, D),
        "bias2": get("L0_gnn_b2").reshape(1, D),
    }
    arrays = {name: np.ascontiguousarray(a) for name, a in arrays.items()}

    nc = bacc.Bacc("TRN2", target_bir_lowering=False, num_devices=1)
    ap = {name: nc.dram_tensor(name, a.shape, mybir.dt.from_np(a.dtype), kind="ExternalInput").ap()
          for name, a in arrays.items()}
    out = nc.dram_tensor("out", (NODE_ROWS, D), mybir.dt.float32, kind="ExternalOutput").ap()
    build(nc, ap["x_rows"], ap["meta"], ap["hot_src"], ap["ea_t"], ap["dst_runs"], ap["prev_last"], ap["dst_rows"],
          ap["row_last"], [ap["w_node1"], ap["w_node2"]], [ap["w_edge1"], ap["w_edge2"]],
          [ap["bias1"], ap["bias2"]], out)
    r = run_bass_kernel_spmd(nc, [arrays], core_ids=[0])
    return r.results[0]["out"][:N_NODES]
```

```python
import concourse.bass as bass
from concourse import mybir
from contextlib import ExitStack

P = 128
N_NODES, N_EDGES, D, DE = 6250, 200000, 96, 32

NODE_CHUNK = 5
NODE_CHUNKS = 10
NODE_TILES = NODE_CHUNK * NODE_CHUNKS
NODE_ROWS = P * NODE_TILES

GROUP = 4
CHUNK_GROUPS = 7
CHUNK = GROUP * CHUNK_GROUPS
CHUNK_FIRST = 20
CHUNKS = 56
STEPS = CHUNK * CHUNKS
EDGE_ROWS = P * STEPS
ROUNDS = CHUNKS // 2
GROUPS = STEPS // GROUP

SEARCH = 448
SEARCH_COLS = NODE_TILES + 1
ROW_BATCHES = ((0, 5, False), (5, 18, True), (18, 26, True), (26, 34, True), (34, 42, False), (42, SEARCH_COLS, False))
SCALAR_FOUND = slice(5, 34)
FIND_BEFORE = (13, 4, 4, 4)
FIND_EACH = 3
VECTOR_COUNTED = 15
HOT = {1: 3, 3: 3, 5: 3}
HOTS = len(HOT)
EDGE_BANKS = (0, 1, 2, 3, 4, 0, 1, 5, 3, 2, 0, 1, 4, 5)


def bank_age(place):
    return next(n for n in range(1, len(EDGE_BANKS) + 1) if EDGE_BANKS[place - n] == EDGE_BANKS[place])


META = 2 * CHUNK + 1
assert SEARCH * SEARCH == EDGE_ROWS
ROWS_UNDER = -(-(HOTS + 1) * NODE_TILES * P // (2 * SEARCH))

BIG = 3.4e38
EPS = 1e-5
SLOPE = 0.01


def build(nc, x, meta, hot_src, ea_t, dst_runs, prev_last, dst_rows, row_last, w_nodes, w_edges, biases, out):
    fp32, bf16, i32 = mybir.dt.float32, mybir.dt.bfloat16, mybir.dt.int32
    ALU, ACT, AX = mybir.AluOpType, mybir.ActivationFunctionType, mybir.AxisListType

    y_table = nc.dram_tensor("y_table", (NODE_ROWS, D), fp32, kind="Internal").ap()
    maxima = nc.dram_tensor("maxima", (EDGE_ROWS + 1, D), fp32, kind="Internal").ap()
    maxima_runs = maxima[0:EDGE_ROWS, :].rearrange("(p t) d -> p (t d)", p=P)
    y_runs = y_table.rearrange("(p k) d -> p (k d)", p=P)

    with ExitStack() as ctx:
        def sb(name, shape, dt=fp32):
            return ctx.enter_context(nc.sbuf_tensor(name, shape, dt))

        def sem(name):
            return ctx.enter_context(nc.semaphore(name))

        root_sb = sb("root_sb", [P, NODE_TILES * D])
        ring = sb("ring", [P, 2 * CHUNK * D])
        x_sb = ring[:, 0:NODE_TILES * D]
        squares = x_sb
        h_all = x_sb
        ea = sb("ea", [P, 2, CHUNK_GROUPS * P])
        meta_sb = sb("meta_sb", [P, 2, META], i32)
        same = sb("same", [P, 2, CHUNK])
        cut = sb("cut", [P, 2, CHUNK])
        y_parts = sb("y_parts", [P, NODE_TILES, 3, D], bf16)
        y_flat = y_parts[:, :, :, :].rearrange("p k s d -> p (k s d)")
        dst_sb = y_flat[:, 0:2 * STEPS].bitcast(i32)
        dst_junk = y_flat[:, 2 * STEPS:3 * STEPS]
        prev_sb = sb("prev_sb", [P, 1], i32)
        search_space = sb("search_space", [P, SEARCH_COLS * SEARCH], i32)
        rows_sb = search_space[:, :].rearrange("p (k c) -> p k c", c=SEARCH)
        wide = search_space[:, 0:(HOTS + 1) * NODE_TILES * P // 2].bitcast(bf16).rearrange(
            "p (q k e) -> p q k e", k=NODE_TILES, e=P)
        tile_no = wide[:, HOTS, :, :]
        tile_row_i = sb("tile_row_i", [P, NODE_TILES], i32)
        tile_row = sb("tile_row", [P, NODE_TILES], bf16)
        hot_sb = sb("hot_sb", [P, 2, HOTS * P], i32)
        hot_tile = sb("hot_tile", [P, 2, HOTS * P], bf16)
        minus_base = sb("minus_base", [P, 1])
        rest = sb("rest", [P, 2, NODE_CHUNK * D])
        row_last_sb = sb("row_last_sb", [P, SEARCH], i32)
        junk_act = sb("junk_act", [P, 2, SEARCH], mybir.dt.bfloat16)
        junk_dve = sb("junk_dve", [P, SEARCH], bf16)
        node_id_i = sb("node_id_i", [P, SEARCH_COLS], i32)
        node_id = sb("node_id", [P, SEARCH_COLS])
        node_mid = sb("node_mid", [P, SEARCH_COLS])
        signs = sb("signs", [P, SEARCH_COLS])
        row_f = sb("row_f", [P, SEARCH_COLS])
        row_i = sb("row_i", [P, SEARCH_COLS], i32)
        in_row = sb("in_row", [P, SEARCH_COLS])
        ends = sb("ends", [P, SEARCH_COLS])
        has_edges = sb("has_edges", [P, NODE_TILES])
        agg_row_f = sb("agg_row_f", [P, NODE_TILES])
        agg_row = sb("agg_row", [P, NODE_TILES], i32)
        agg_idx = sb("agg_idx", [P, 2, NODE_CHUNK], i32)
        agg = sb("agg", [P, 2, NODE_CHUNK * D])
        h = sb("h", [P, 2, NODE_CHUNK * D])
        hT = sb("hT", [D + 1, 2, NODE_CHUNK * P])
        y_sb = sb("y_sb", [P, 2, NODE_CHUNK * D])
        x_again = rest
        res = y_sb
        hot_parts = y_sb[:, :, :].rearrange("p a c -> p (a c)")[:, 0:HOTS * 3 * D].rearrange(
            "p (q c) -> p q c", q=HOTS)
        stats = sb("stats", [P, 4, NODE_TILES])
        ident = sb("ident", [P, P])
        w_node_sb = sb("w_node_sb", [D + 1, 2, 2 * D])
        w_edge_sb = sb("w_edge_sb", [P, 2, GROUP * D])
        zero_row = sb("zero_row", [1, D])
        zero_state = sb("zero_state", [P, D])
        run_base_i = sb("run_base_i", [P, 1], i32)
        run_base = sb("run_base", [P, 1])
        dst_first = sb("dst_first", [P, 1])
        first_len = sb("first_len", [P, 1])
        goes_on = sb("goes_on", [P, 1])
        carry_cut = sb("carry_cut", [P, 1])
        one_segment = sb("one_segment", [P, 1])
        through = sb("through", [P, 1])
        through_cut = sb("through_cut", [P, D])
        through_cutT = sb("through_cutT", [D, P])
        patch_row_f = sb("patch_row_f", [P, 1])
        patch_row = sb("patch_row", [P, 1], i32)
        carryT = sb("carryT", [D, P + 1])
        patch_in = sb("patch_in", [P, D])
        patched = sb("patched", [P, D])

        psum = ctx.enter_context(nc.psum_tensor("psum", [P, 8 * 512], fp32))

        def edge_bank(slot):
            return psum[:, 512 * EDGE_BANKS[slot]:512 * EDGE_BANKS[slot] + GROUP * D]

        def hot_bank(half, q):
            bank = 6 + (half * HOTS + q) % 2
            return psum[:, 512 * bank:512 * bank + 3 * D]

        def hT_ps(half):
            return psum[0:D, 3072 * half:3072 * half + NODE_CHUNK * P]

        def node_ps(half, term):
            bank = 2 + 2 * half + term
            return psum[:, 512 * bank:512 * bank + NODE_CHUNK * D]

        lastT_ps = psum[0:D, 3584:3584 + P]
        carry_ps = psum[:, 3584 + P:3584 + P + D]

        x_in = [sem("x_in0"), sem("x_in1")]
        ident_zeroed = sem("ident_zeroed")
        ident_ready = sem("ident_ready")
        blocks_zeroed = sem("blocks_zeroed")
        w_in = sem("w_in")
        zero_ready = sem("zero_ready")
        ones_ready = sem("ones_ready")
        zero_stored = sem("zero_stored")
        search_in = sem("search_in")
        dst_in = sem("dst_in")
        pool_chain = sem("pool_chain")
        mids_ready = sem("mids_ready")
        rows_counted = sem("rows_counted")
        signs_ready = sem("signs_ready")
        rows_found = sem("rows_found")
        rows_in = [sem(f"rows_in{b}") for b in range(len(ROW_BATCHES))]
        dve_chain = sem("dve_chain")
        centred = sem("centred")
        squared = sem("squared")
        var_ready = sem("var_ready")
        std_ready = sem("std_ready")
        agg_rows_ready = sem("agg_rows_ready")
        through_ready = sem("through_ready")
        throughT_ready = sem("throughT_ready")
        throughT_copied = sem("throughT_copied")
        patch_row_ready = sem("patch_row_ready")
        h_ready = sem("h_ready")
        hT_ready = sem("hT_ready")
        hT_copied = sem("hT_copied")
        y_ready = sem("y_ready")
        root_ready = sem("root_ready")
        y_copied = sem("y_copied")
        y_stored = [sem("y_stored0"), sem("y_stored1")]
        root_stored = sem("root_stored")
        meta_in = [sem("meta_in0"), sem("meta_in1")]
        ea_in = [sem("ea_in0"), sem("ea_in1")]
        gathered = [sem(f"gathered{s}") for s in range(2 * CHUNK_GROUPS)]
        edge_ready = sem("edge_ready")
        hot_ready = sem("hot_ready")
        hot_copied = sem("hot_copied")
        hot_msg_ready = sem("hot_msg_ready")
        same_ready = sem("same_ready")
        cut_ready = sem("cut_ready")
        msg_ready = sem("msg_ready")
        steps_done = sem("steps_done")
        maxima_stored = [sem("maxima_stored0"), sem("maxima_stored1")]
        lastT_ready = sem("lastT_ready")
        carryT_ready = sem("carryT_ready")
        carry_ready = sem("carry_ready")
        patch_in_ready = sem("patch_in_ready")
        patched_ready = sem("patched_ready")
        patch_stored = sem("patch_stored")
        idx_ready = sem("idx_ready")
        agg_in = [sem("agg_in0"), sem("agg_in1")]
        updated = sem("updated")
        x_again_in = [sem("x_again_in0"), sem("x_again_in1")]
        hot_in = [sem("hot_in0"), sem("hot_in1")]
        hot_tile_ready = sem("hot_tile_ready")
        onehot_ready = sem("onehot_ready")
        tile_no_ready = sem("tile_no_ready")
        y_hi_ready = sem("y_hi_ready")
        rest_ready = sem("rest_ready")
        y_mid_ready = sem("y_mid_ready")
        y_parts_ready = sem("y_parts_ready")
        sum_ready = sem("sum_ready")
        res_ready = sem("res_ready")
        out_stored = [sem("out_stored0"), sem("out_stored1")]

        block = ctx.enter_context(nc.Block())

        def rounds(eng, layer, body, after_first=None):
            if layer == 0:
                body(0, 0)
                if after_first:
                    after_first()
                with eng.Fori(1, ROUNDS) as i:
                    body(i, i)
            else:
                with eng.Fori(0, ROUNDS) as i:
                    body(i, i + ROUNDS)

        def node_rounds(eng, stage, body):
            n = NODE_CHUNKS // 2
            if stage == 0:
                body(0, 0)
                with eng.Fori(1, n) as i:
                    body(i, i)
            else:
                with eng.Fori(0, n) as i:
                    body(i, i + n * stage)

        def past(n):
            return not (isinstance(n, int) and n < 1)

        def ring_chunk(half):
            return ring[:, half * CHUNK * D:(half + 1) * CHUNK * D]

        def ring_group(slot):
            return ring[:, slot * GROUP * D:(slot + 1) * GROUP * D]

        def ring_step(slot, j):
            at = (slot * GROUP + j) * D
            return ring[:, at:at + D]

        def x_part(part, width=D):
            return slice(part * NODE_TILES // 2 * width, (part + 1) * NODE_TILES // 2 * width)

        @block.sync
        def _(sp):
            sp.dma_start(row_last_sb[:, :], row_last.to_broadcast((P, SEARCH))).then_inc(search_in, 16)
            for part in range(2):
                sp.dma_start(x_sb[:, x_part(part)], x.rearrange("(p k) d -> p (k d)", p=P)[:, x_part(part)]
                             ).then_inc(x_in[part], 16)
            sp.dma_start(dst_sb, dst_runs).then_inc(dst_in, 16)
            sp.dma_start(prev_sb[:, :], prev_last).then_inc(dst_in, 16)
            for layer in range(2):
                sp.dma_start(w_node_sb[0:D, layer, :], w_nodes[layer]).then_inc(w_in, 16)
                sp.dma_start(w_node_sb[D:D + 1, layer, D:2 * D], biases[layer]).then_inc(w_in, 16)
            sp.wait_ge(blocks_zeroed, 1)
            for layer in range(2):
                for j in range(GROUP):
                    sp.dma_start(w_edge_sb[j * DE:(j + 1) * DE, layer, j * D:(j + 1) * D],
                                 w_edges[layer]).then_inc(w_in, 16)
            sp.wait_ge(zero_ready, 1)
            sp.dma_start(maxima[EDGE_ROWS:EDGE_ROWS + 1, :], zero_row[:, :]).then_inc(zero_stored, 16)

            def load_hot(c, half):
                sp.dma_start(hot_sb[:, half, :], hot_src[c, :, :].rearrange("a b c -> (a b) c")
                             .to_broadcast((P, HOTS * P))).then_inc(hot_in[half], 16)

            def load_edges(c, half):
                sp.dma_start(meta_sb[:, half, :], meta[c, :, :].rearrange("a p c -> (a p) c")
                             ).then_inc(meta_in[half], 16)
                sp.dma_start(ea[:, half, :], ea_t[c, :, :].rearrange("a p c -> (a p) c")
                             ).then_inc(ea_in[half], 16)

            for half in range(2):
                load_hot(slice(half, half + 1), half)
                load_edges(slice(half, half + 1), half)

            def store_y(i, m):
                for half in range(2):
                    sp.wait_ge(y_copied, 2 * m + half + 1)
                    sp.dma_start(y_runs[:, bass.ds((2 * i + half) * (NODE_CHUNK * D), NODE_CHUNK * D)],
                                 y_sb[:, half, :]).then_inc(y_stored[half], 16)

            def edge_round(i, m):
                for half in range(2):
                    sp.wait_ge(hot_tile_ready, 2 * m + half + 1)
                    load_hot(bass.ds(2 * i + half + 2, 1), half)
                    for first, end in ((0, CHUNK_FIRST), (CHUNK_FIRST, CHUNK)):
                        sp.wait_ge(steps_done, CHUNK * (2 * m + half) + end)
                        sp.dma_start(maxima_runs[:, bass.ds(((2 * i + half) * CHUNK + first) * D, (end - first) * D)],
                                     ring_chunk(half)[:, first * D:end * D]).then_inc(maxima_stored[half], 16)
                    load_edges(bass.ds(2 * i + half + 2, 1), half)

            for layer in range(2):
                node_rounds(sp, layer, store_y)
                rounds(sp, layer, edge_round)
            for half in range(2):
                sp.wait_ge(maxima_stored[half], 32 * 2 * ROUNDS)
                sp.wait_ge(meta_in[half], 16 * (2 * ROUNDS + 1))
                sp.wait_ge(ea_in[half], 16 * (2 * ROUNDS + 1))
                sp.wait_ge(hot_in[half], 16 * (2 * ROUNDS + 1))

            x_runs = x.rearrange("(p k) d -> p (k d)", p=P)
            out_runs = out.rearrange("(p k) d -> p (k d)", p=P)

            sp.wait_ge(y_parts_ready, 2 * NODE_CHUNKS)

            def store_round(i, m):
                for half in range(2):
                    if past(i):
                        sp.wait_ge(res_ready, 2 * i + half - 1)
                    sp.dma_start(x_again[:, half, :],
                                 x_runs[:, bass.ds((2 * i + half) * (NODE_CHUNK * D), NODE_CHUNK * D)]
                                 ).then_inc(x_again_in[half], 16)
                for half in range(2):
                    sp.wait_ge(res_ready, 2 * i + half + 1)
                    sp.dma_start(out_runs[:, bass.ds((2 * i + half) * (NODE_CHUNK * D), NODE_CHUNK * D)],
                                 res[:, half, :]).then_inc(out_stored[half], 16)

            store_round(0, 0)
            with sp.Fori(1, NODE_CHUNKS // 2) as i:
                store_round(i, i)
            for half in range(2):
                sp.wait_ge(out_stored[half], 16 * (NODE_CHUNKS // 2))

        @block.gpsimd
        def _(pool):
            links = [0]

            def link(ins):
                links[0] += 1
                ins.then_inc(pool_chain, 1)
                pool.wait_ge(pool_chain, links[0])

            link(pool.iota(node_id_i[:, :], pattern=[[1, SEARCH_COLS]], base=-1, channel_multiplier=NODE_TILES))
            link(pool.tensor_copy(node_id[:, :], node_id_i[:, :]))
            pool.tensor_scalar(node_mid[:, :], node_id[:, :], 0.5, None, ALU.add).then_inc(mids_ready, 1)
            link(pool.iota(run_base_i[:, :], pattern=[[0, 1]], base=0, channel_multiplier=STEPS))
            pool.tensor_copy(run_base[:, :], run_base_i[:, :]).then_inc(mids_ready, 1)
            pool.tensor_scalar(minus_base[:, :], node_id[:, 0:1], 1.0, -1.0, ALU.add, ALU.mult).then_inc(mids_ready, 1)
            link(pool.iota(tile_row_i[:, :], pattern=[[1, NODE_TILES]], base=0, channel_multiplier=0))
            pool.tensor_copy(tile_row[:, :], tile_row_i[:, :]).then_inc(mids_ready, 1)
            pool.memset(w_edge_sb[:, :, :], 0.0).then_inc(blocks_zeroed, 1)
            pool.memset(zero_row[:, :], 0.0).then_inc(zero_ready, 1)
            pool.memset(ident[:, :], 0.0).then_inc(ident_zeroed, 1)
            pool.wait_ge(ident_zeroed, 1)
            pool.affine_select(out=ident[:, :], in_=ident[:, :], compare_op=ALU.not_equal, fill=1.0,
                               base=0, pattern=[[-1, P]], channel_multiplier=1).then_inc(ident_ready, 1)
            ordered = 0
            for b, (first, end, by_scalar) in enumerate(ROW_BATCHES):
                cols = slice(first, end)
                if by_scalar:
                    pool.wait_ge(signs_ready, end - SCALAR_FOUND.start)
                    pool.tensor_scalar(row_f[:, cols], signs[:, cols], 0.5, SEARCH / 2,
                                       ALU.mult, ALU.add).then_inc(rows_found, 1)
                    ordered += 1
                    pool.wait_ge(rows_found, ordered)
                else:
                    scalar_before = SCALAR_FOUND.stop - SCALAR_FOUND.start if b else 0
                    pool.wait_ge(rows_counted, end - scalar_before)
                pool.tensor_copy(row_i[:, cols], row_f[:, cols]).then_inc(rows_found, 1)
                ordered += 1
                pool.wait_ge(rows_found, ordered)
                for k in range(first, end):
                    pool.indirect_dma_start(
                        out=rows_sb[:, k, :], out_offset=None, in_=dst_rows[:, :],
                        in_offset=bass.IndirectOffsetOnAxis(ap=row_i[:, k:k + 1], axis=0),
                    ).then_inc(rows_in[b], 16)

            def gather_edges(layer):
                for half in range(2):
                    pool.wait_ge(y_stored[half], 16 * (NODE_CHUNKS // 2) * (layer + 1))

                def gather_round(i, m):
                    for half in range(2):
                        pool.wait_ge(meta_in[half], 16 * (m + 1))
                        if past(m):
                            pool.wait_ge(maxima_stored[half], 32 * m)
                            pool.wait_ge(steps_done, GROUP * (CHUNK_GROUPS * (2 * m + half - 1) + 1))
                        pool.nop(nofuse=True)
                        for g in range(CHUNK_GROUPS):
                            slot = half * CHUNK_GROUPS + g
                            for j in range(GROUP):
                                if HOT.get(g) == j:
                                    continue
                                t = g * GROUP + j
                                pool.indirect_dma_start(
                                    out=ring_step(slot, j), out_offset=None, in_=y_table[:, :],
                                    in_offset=bass.IndirectOffsetOnAxis(ap=meta_sb[:, half, t:t + 1], axis=0),
                                ).then_inc(gathered[slot], 16)

                rounds(pool, layer, gather_round)

            def patch_runs(layer):
                for half in range(2):
                    pool.wait_ge(maxima_stored[half], 32 * ROUNDS * (layer + 1))
                pool.wait_ge(patch_row_ready, 1)
                if layer:
                    pool.wait_ge(patch_stored, 16 * layer)
                pool.indirect_dma_start(
                    out=patch_in[:, :], out_offset=None, in_=maxima[:, :],
                    in_offset=bass.IndirectOffsetOnAxis(ap=patch_row[:, 0:1], axis=0),
                ).then_inc(patch_in_ready, 16)
                pool.wait_ge(patched_ready, layer + 1)
                pool.indirect_dma_start(
                    out=maxima[:, :], out_offset=bass.IndirectOffsetOnAxis(ap=patch_row[:, 0:1], axis=0),
                    in_=patched[:, :], in_offset=None,
                ).then_inc(patch_stored, 16)
                pool.wait_ge(patch_stored, 16 * (layer + 1))

            def gather_aggregates(layer):
                pool.wait_ge(agg_rows_ready, 1)
                pool.wait_ge(zero_stored, 16)

                def agg_round(i, m):
                    n = m - NODE_CHUNKS // 2
                    for half in range(2):
                        wait_free(n, half)
                        pool.tensor_copy(agg_idx[:, half, :],
                                         agg_row[:, bass.ds((2 * i + half) * NODE_CHUNK, NODE_CHUNK)]
                                         ).then_inc(idx_ready, 1)
                        pool.wait_ge(idx_ready, 2 * n + half + 1)
                        pool.nop(nofuse=True)
                        for k in range(NODE_CHUNK):
                            pool.indirect_dma_start(
                                out=agg[:, half, k * D:(k + 1) * D], out_offset=None, in_=maxima[:, :],
                                in_offset=bass.IndirectOffsetOnAxis(ap=agg_idx[:, half, k:k + 1], axis=0),
                            ).then_inc(agg_in[half], 16)

                def wait_free(n, half):
                    if past(n):
                        pool.wait_ge(updated, 2 * n + half - 1)

                r = NODE_CHUNKS // 2
                if layer == 0:
                    agg_round(0, r)
                    with pool.Fori(1, r) as i:
                        agg_round(i, i + r)
                else:
                    with pool.Fori(0, r) as i:
                        agg_round(i, i + 2 * r)

            for layer in range(2):
                gather_edges(layer)
                patch_runs(layer)
                gather_aggregates(layer)

        @block.scalar
        def _(act):
            act.wait_ge(search_in, 16)
            act.wait_ge(mids_ready, 1)
            signed = [0]

            def count_signs(bias, values, k, total):
                n = signed[0]
                if n >= 2:
                    act.wait_ge(signs_ready, n - 1)
                signed[0] += 1
                nc.scalar.activation(junk_act[:, n % 2, :], values, ACT.Sign, scale=-1.0,
                                     bias=bias[:, k:k + 1], accum_out=total[:, k:k + 1]).then_inc(signs_ready, 1)

            def find_rows(first, end):
                for k in range(first, end):
                    count_signs(node_mid, row_last_sb[:, :], k, signs)

            def search_rows(first, end):
                for k in range(first, end):
                    for b, batch in enumerate(ROW_BATCHES):
                        if k == max(first, batch[0]) and k < batch[1]:
                            act.wait_ge(rows_in[b], 16 * (batch[1] - batch[0]))
                    count_signs(node_mid, rows_sb[:, k, :], k, in_row)

            found = SCALAR_FOUND.start
            for part, more in enumerate(FIND_BEFORE[:3]):
                find_rows(found, found + more)
                found += more
                if part < 2:
                    act.wait_ge(centred, part + 1)
                    nc.scalar.activation(squares[:, x_part(part)], root_sb[:, x_part(part)],
                                         ACT.Square).then_inc(squared, 1)
            act.wait_ge(var_ready, 1)
            nc.scalar.activation(stats[:, 2, :], stats[:, 1, :], ACT.Sqrt).then_inc(std_ready, 1)
            find_rows(found, found + FIND_BEFORE[3])
            found += FIND_BEFORE[3]
            act.wait_ge(throughT_ready, 1)
            nc.scalar.copy(through_cutT[:, :], lastT_ps).then_inc(throughT_copied, 1)
            act.wait_ge(mids_ready, 3)

            def place_hot(half):
                nc.scalar.activation(hot_tile[:, half, :], hot_sb[:, half, :], ACT.Identity,
                                     bias=minus_base[:, 0:1]).then_inc(hot_tile_ready, 1)

            act.wait_ge(hot_in[0], 16)
            place_hot(0)
            find_rows(found, SCALAR_FOUND.stop)

            def node_copies(stage):
                def copy_hT(half, n):
                    act.wait_ge(hT_ready, n + 1)
                    if past(n - 1):
                        act.wait_ge(root_ready, n - 1)
                    nc.scalar.copy(hT[0:D, half, :], hT_ps(half)).then_inc(hT_copied, 1)

                def copy_y(half, n):
                    act.wait_ge(y_ready, n + 1)
                    if past(n - 1):
                        act.wait_ge(y_stored[half], 8 * (n - half))
                        act.wait_ge(rest_ready, n - 1)
                    nc.scalar.copy(y_sb[:, half, :], node_ps(half, 0)).then_inc(y_copied, 1)

                def copy_hi(half, n, i):
                    its_tiles = bass.ds((2 * i + half) * NODE_CHUNK, NODE_CHUNK)
                    act.wait_ge(y_copied, n + 1)
                    nc.scalar.copy(y_parts[:, its_tiles, 0, :],
                                   y_sb[:, half, :].rearrange("p (k c) -> p k c", c=D)).then_inc(y_hi_ready, 1)

                def copy_root(half, n, i):
                    cols = bass.ds((2 * i + half) * (NODE_CHUNK * D), NODE_CHUNK * D)
                    act.wait_ge(root_ready, n + 1)
                    if stage == 0:
                        act.wait_ge(h_ready, NODE_CHUNKS)
                    nc.scalar.copy(root_sb[:, cols], node_ps(half, 1)).then_inc(root_stored, 1)

                def copy_round(i, m):
                    for half in range(2):
                        copy_hT(half, 2 * m + half)
                    for half in range(2):
                        copy_y(half, 2 * m + half)
                        copy_hi(half, 2 * m + half, i)
                    for half in range(2):
                        copy_root(half, 2 * m + half, i)

                if stage == 0:
                    for half in range(2):
                        copy_hT(half, half)
                    for n in range(NODE_CHUNKS):
                        copy_y(n % 2, n)
                        copy_hi(n % 2, n, n // 2)
                        if n + 2 < NODE_CHUNKS:
                            copy_hT(n % 2, n + 2)
                        copy_root(n % 2, n, n // 2)
                else:
                    node_rounds(act, stage, copy_round)

            def hot_copies(layer):
                for half in range(2):
                    act.wait_ge(y_stored[half], 16 * (NODE_CHUNKS // 2) * (layer + 1))

                def hot_round(i, m):
                    for half in range(2):
                        act.wait_ge(hot_in[1 - half], 16 * (m + 1 + half))
                        if past(2 * m + half):
                            act.wait_ge(onehot_ready, HOTS * (2 * m + half))
                        place_hot(1 - half)
                        for q in range(HOTS):
                            hots = HOTS * (2 * m + half) + q + 1
                            act.wait_ge(hot_ready, hots)
                            if past(hots - HOTS):
                                act.wait_ge(hot_msg_ready, hots - HOTS)
                            nc.scalar.copy(hot_parts[:, q, :], hot_bank(half, q)).then_inc(hot_copied, 1)

                rounds(act, layer, hot_round, (lambda: search_rows(ROWS_UNDER, SEARCH_COLS)) if layer == 0 else None)

            node_copies(0)
            search_rows(VECTOR_COUNTED, ROWS_UNDER)
            act.wait_ge(signs_ready, signed[0])
            nc.scalar.copy(tile_no, tile_row[:, :].unsqueeze(2).to_broadcast((P, NODE_TILES, P))
                           ).then_inc(tile_no_ready, 1)
            hot_copies(0)
            node_copies(1)
            hot_copies(1)

        @block.vector
        def _(dve):
            links = [0]

            def link(ins):
                links[0] += 1
                ins.then_inc(dve_chain, 1)
                dve.wait_ge(dve_chain, links[0])

            def tiles(ap):
                return ap.rearrange("p (k c) -> p k c", c=D)

            def per_tile(ap, n=NODE_TILES):
                return ap.unsqueeze(2).to_broadcast((P, n, D))

            mean, var, std, rstd = (stats[:, s, :] for s in range(4))
            nc.vector.memset(hT[D:D + 1, :, :], 1.0).then_inc(ones_ready, 1)
            dve.wait_ge(search_in, 16)
            dve.wait_ge(mids_ready, 1)
            def find_rows(first, end):
                for k in range(first, end):
                    nc.vector.tensor_scalar(junk_dve[:, :], row_last_sb[:, :], node_id[:, k:k + 1], 0.0,
                                            ALU.is_le, ALU.add, accum_out=row_f[:, k:k + 1]).then_inc(rows_counted, 1)
                    scalar_before = SCALAR_FOUND.stop - SCALAR_FOUND.start if k >= SCALAR_FOUND.stop else 0
                    dve.wait_ge(rows_counted, k + 1 - scalar_before)

            find_rows(0, SCALAR_FOUND.start)
            for part in range(2):
                of = mean[:, x_part(part, 1)]
                dve.wait_ge(x_in[part], 16)
                link(nc.vector.tensor_reduce(of, tiles(x_sb[:, x_part(part)]), axis=AX.X, op=ALU.add))
                link(nc.vector.tensor_scalar(of, of, 1.0 / D, None, ALU.mult))
                nc.vector.tensor_tensor(tiles(root_sb[:, x_part(part)]), tiles(x_sb[:, x_part(part)]),
                                        per_tile(of, NODE_TILES // 2), ALU.subtract).then_inc(centred, 1)
            for part in range(2):
                dve.wait_ge(squared, part + 1)
                link(nc.vector.tensor_reduce(var[:, x_part(part, 1)], tiles(squares[:, x_part(part)]),
                                             axis=AX.X, op=ALU.add))
            nc.vector.tensor_scalar(var, var, 1.0 / D, EPS, ALU.mult, ALU.add).then_inc(var_ready, 1)
            dve.wait_ge(dst_in, 32)
            dve.wait_ge(mids_ready, 4)
            link(nc.vector.tensor_copy(dst_first[:, :], dst_sb[:, 0:1]))
            link(nc.vector.tensor_scalar(dst_junk, dst_sb, dst_first[:, 0:1], 0.0, ALU.is_equal,
                                         ALU.add, accum_out=first_len[:, :]))
            link(nc.vector.tensor_tensor(goes_on[:, :], prev_sb[:, :], dst_first[:, :], ALU.is_equal))
            link(nc.vector.tensor_scalar(carry_cut[:, :], goes_on[:, :], -1.0, BIG, ALU.add, ALU.mult))
            link(nc.vector.tensor_scalar(one_segment[:, :], first_len[:, :], float(STEPS), None, ALU.is_equal))
            link(nc.vector.tensor_tensor(through[:, :], goes_on[:, :], one_segment[:, :], ALU.mult))
            link(nc.vector.tensor_scalar(through[:, :], through[:, :], -1.0, BIG, ALU.add, ALU.mult))
            nc.vector.tensor_copy(through_cut[:, :], through[:, 0:1].to_broadcast((P, D))).then_inc(through_ready, 1)
            link(nc.vector.scalar_tensor_tensor(patch_row_f[:, :], first_len[:, :], -1.0, run_base[:, :],
                                                ALU.add, ALU.add))
            nc.vector.tensor_copy(patch_row[:, :], patch_row_f[:, :]).then_inc(patch_row_ready, 1)
            link(nc.vector.memset(carryT[:, 0:1], 0.0))
            link(nc.vector.memset(zero_state[:, :], 0.0))

            dve.wait_ge(std_ready, 1)
            link(nc.vector.reciprocal(rstd, std))

            def split_y(half, n, c):
                its_tiles = bass.ds(c * NODE_CHUNK, NODE_CHUNK)
                dve.wait_ge(y_hi_ready, n + 1)
                nc.vector.tensor_tensor(tiles(rest[:, half, :]), tiles(y_sb[:, half, :]),
                                        y_parts[:, its_tiles, 0, :], ALU.subtract).then_inc(rest_ready, 1)
                dve.wait_ge(rest_ready, n + 1)
                nc.vector.tensor_copy(y_parts[:, its_tiles, 1, :], tiles(rest[:, half, :])
                                      ).then_inc(y_mid_ready, 1)
                dve.wait_ge(y_mid_ready, n + 1)
                nc.vector.tensor_tensor(y_parts[:, its_tiles, 2, :], tiles(rest[:, half, :]),
                                        y_parts[:, its_tiles, 1, :], ALU.subtract).then_inc(y_parts_ready, 1)

            with dve.Fori(0, NODE_CHUNKS) as i:
                cols = bass.ds(i * (NODE_CHUNK * D), NODE_CHUNK * D)
                nc.vector.scalar_tensor_tensor(
                    tiles(h_all[:, cols]), tiles(root_sb[:, cols]), 0.0,
                    per_tile(stats[:, 3, bass.ds(i * NODE_CHUNK, NODE_CHUNK)], NODE_CHUNK),
                    ALU.max, ALU.mult).then_inc(h_ready, 1)

            def build_onehot(q, half, built):
                dve.wait_ge(hot_tile_ready, built)
                nc.vector.tensor_tensor(
                    wide[:, q, :, :],
                    hot_tile[:, half, q * P:(q + 1) * P].unsqueeze(1).to_broadcast((P, NODE_TILES, P)),
                    tile_no, ALU.is_equal).then_inc(onehot_ready, 1)

            def count_in_first_rows():
                for k in range(VECTOR_COUNTED):
                    for b, (first, end, _) in enumerate(ROW_BATCHES):
                        if k == first:
                            dve.wait_ge(rows_in[b], 16 * (end - first))
                    link(nc.vector.tensor_scalar(junk_dve[:, :], rows_sb[:, k, :], node_id[:, k:k + 1], 0.0,
                                                 ALU.is_le, ALU.add, accum_out=in_row[:, k:k + 1]))

            def find_ends():
                dve.wait_ge(signs_ready, SCALAR_FOUND.stop - SCALAR_FOUND.start + SEARCH_COLS - VECTOR_COUNTED)
                others = in_row[:, VECTOR_COUNTED:]
                link(nc.vector.tensor_scalar(others, others, 0.5, SEARCH / 2, ALU.mult, ALU.add))
                link(nc.vector.scalar_tensor_tensor(ends[:, :], row_f[:, :], float(SEARCH), in_row[:, :],
                                                    ALU.mult, ALU.add))
                link(nc.vector.tensor_tensor(has_edges[:, :], ends[:, 1:], ends[:, 0:NODE_TILES], ALU.is_gt))
                link(nc.vector.scalar_tensor_tensor(agg_row_f[:, :], ends[:, 1:], -1.0 - EDGE_ROWS,
                                                    has_edges[:, :], ALU.add, ALU.mult))
                link(nc.vector.tensor_scalar(agg_row_f[:, :], agg_row_f[:, :], float(EDGE_ROWS), None, ALU.add))
                nc.vector.tensor_copy(agg_row[:, :], agg_row_f[:, :]).then_inc(agg_rows_ready, 1)

            def reduce_edges(layer):
                def edge_round(i, m):
                    for half in range(2):
                        dve.wait_ge(meta_in[half], 16 * (m + 1))
                        nc.vector.tensor_tensor(same[:, half, :], meta_sb[:, half, CHUNK:2 * CHUNK],
                                                meta_sb[:, half, CHUNK + 1:META], ALU.is_equal).then_inc(same_ready, 1)
                        dve.wait_ge(same_ready, 2 * m + half + 1)
                        nc.vector.tensor_scalar(cut[:, half, :], same[:, half, :], -1.0, BIG,
                                                ALU.add, ALU.mult).then_inc(cut_ready, 1)
                        dve.wait_ge(cut_ready, 2 * m + half + 1)
                        own_messages(m, half, 0)
                        for g in range(CHUNK_GROUPS):
                            scan_step(m, half, g, 0)
                            scan_step(m, half, g, 1)
                            if g + 1 in HOT:
                                hot_message(m, half, g + 1)
                            scan_step(m, half, g, 2)
                            if g + 1 < CHUNK_GROUPS:
                                own_messages(m, half, g + 1)
                            scan_step(m, half, g, 3)
                            if g in HOT and g != max(HOT):
                                build_onehot(list(HOT).index(g), 1 - half, 2 * m + half + 2)
                        build_onehot(HOTS - 1, 1 - half, 2 * m + half + 2)

                def own_messages(m, half, g):
                    slot = half * CHUNK_GROUPS + g
                    own = GROUP * D if g not in HOT else HOT[g] * D
                    dve.wait_ge(gathered[slot], 16 * (GROUP - (g in HOT)) * (m + 1))
                    dve.wait_ge(edge_ready, CHUNK_GROUPS * (2 * m + half) + g + 1)
                    nc.vector.tensor_tensor(ring_group(slot)[:, 0:own], ring_group(slot)[:, 0:own],
                                            edge_bank(slot)[:, 0:own], ALU.add).then_inc(msg_ready, 1)

                def hot_message(m, half, g):
                    q = list(HOT).index(g)
                    dve.wait_ge(hot_copied, HOTS * (2 * m + half) + q + 1)
                    nc.vector.tensor_reduce(
                        ring_step(half * CHUNK_GROUPS + g, HOT[g]),
                        hot_parts[:, q, :].rearrange("p (s d) -> p d s", s=3),
                        axis=AX.X, op=ALU.add).then_inc(hot_msg_ready, 1)

                def scan_step(m, half, g, j):
                    slot = half * CHUNK_GROUPS + g
                    step = CHUNK * (2 * m + half) + g * GROUP + j
                    prev = ring_step(0, (slot * GROUP + j - 1) % (2 * CHUNK))
                    if j == 0:
                        dve.wait_ge(msg_ready, CHUNK_GROUPS * (2 * m + half) + g + 1)
                    if HOT.get(g) == j:
                        dve.wait_ge(hot_msg_ready, HOTS * (2 * m + half) + list(HOT).index(g) + 1)
                    if past(step):
                        dve.wait_ge(steps_done, step)
                    else:
                        prev = zero_state[:, :]
                    nc.vector.scalar_tensor_tensor(
                        ring_step(slot, j), prev, cut[:, half, g * GROUP + j:g * GROUP + j + 1],
                        ring_step(slot, j), ALU.add, ALU.max).then_inc(steps_done, 1)

                rounds(dve, layer, edge_round)
                if layer == 0:
                    find_ends()

            def carry_runs(layer):
                dve.wait_ge(lastT_ready, layer + 1)
                dve.wait_ge(throughT_copied, 1)
                nc.vector.tensor_tensor_scan(carryT[:, 1:P + 1], through_cutT[:, :], lastT_ps, 0.0,
                                             ALU.add, ALU.max).then_inc(carryT_ready, 1)
                dve.wait_ge(carry_ready, layer + 1)
                dve.wait_ge(patch_in_ready, 16 * (layer + 1))
                nc.vector.scalar_tensor_tensor(patched[:, :], carry_ps, carry_cut[:, 0:1], patch_in[:, :],
                                               ALU.add, ALU.max).then_inc(patched_ready, 1)

            def update(stage):
                def update_round(i, m):
                    n = m - NODE_CHUNKS // 2
                    for half in range(2):
                        cols = bass.ds((2 * i + half) * (NODE_CHUNK * D), NODE_CHUNK * D)
                        c = 2 * n + half
                        dve.wait_ge(agg_in[half], 16 * NODE_CHUNK * (n + 1))
                        nc.vector.tensor_tensor(agg[:, half, :], agg[:, half, :], root_sb[:, cols],
                                                ALU.add).then_inc(sum_ready, 1)
                        dve.wait_ge(sum_ready, c + 1)
                        if stage == 1:
                            dve.wait_ge(hT_ready, 2 * m + half - 1)
                        nc.vector.scalar_tensor_tensor(
                            h[:, half, :], agg[:, half, :], SLOPE, agg[:, half, :],
                            ALU.mult, ALU.max).then_inc(updated, 1)
                        if stage == 2:
                            dve.wait_ge(updated, c + 1)
                            dve.wait_ge(x_again_in[half], 16 * (i + 1))
                            if past(i):
                                dve.wait_ge(out_stored[half], 16 * i)
                            nc.vector.tensor_tensor(res[:, half, :], h[:, half, :], x_again[:, half, :],
                                                    ALU.add).then_inc(res_ready, 1)
                        elif half == 1:
                            split_y(0, 2 * m, 2 * i)
                        elif past(i):
                            split_y(1, 2 * m - 1, 2 * i - 1)

                r = NODE_CHUNKS // 2
                dve.wait_ge(root_stored, NODE_CHUNKS * stage)
                update_round(0, r * stage)
                with dve.Fori(1, r) as i:
                    update_round(i, i + r * stage)
                if stage == 1:
                    split_y(1, 2 * NODE_CHUNKS - 1, NODE_CHUNKS - 1)

            for n in range(NODE_CHUNKS):
                first = min(SCALAR_FOUND.stop + FIND_EACH * n, SEARCH_COLS)
                find_rows(first, min(first + FIND_EACH, SEARCH_COLS))
                split_y(n % 2, n, n)
            count_in_first_rows()
            dve.wait_ge(tile_no_ready, 1)
            for q in range(HOTS):
                build_onehot(q, 0, 1)
            reduce_edges(0)
            carry_runs(0)
            update(1)
            reduce_edges(1)
            carry_runs(1)
            update(2)

        @block.tensor
        def _(pe):
            pe.wait_ge(ident_ready, 1)
            pe.wait_ge(ones_ready, 1)
            pe.wait_ge(w_in, 16 * (4 + 2 * GROUP))
            pe.wait_ge(through_ready, 1)
            nc.tensor.transpose(lastT_ps, through_cut[:, :], ident[:, :]).then_inc(throughT_ready, 1)
            pe.wait_ge(throughT_copied, 1)

            def node_products(stage):
                def transposes(half, n):
                    if stage == 0:
                        pe.wait_ge(h_ready, n + 1)
                    else:
                        pe.wait_ge(updated, n - NODE_CHUNKS + 1)
                    if past(n - 1):
                        pe.wait_ge(hT_copied, n - 1)
                    for k in range(NODE_CHUNK):
                        at = k * D + (NODE_CHUNK * D * n if stage == 0 else 0)
                        from_h = h_all[:, at:at + D] if stage == 0 else h[:, half, at:at + D]
                        last = nc.tensor.transpose(hT_ps(half)[:, k * P:(k + 1) * P], from_h, ident[:, :])
                    last.then_inc(hT_ready, 1)

                def products(half, term, n):
                    pe.wait_ge(hT_copied, n + 1)
                    if past(n - 1):
                        pe.wait_ge((y_copied, root_stored)[term], n - 1)
                    for k in range(NODE_CHUNK):
                        rows = slice(0, D + term)
                        last = nc.tensor.matmul(
                            node_ps(half, term)[:, k * D:(k + 1) * D], hT[rows, half, k * P:(k + 1) * P],
                            w_node_sb[rows, stage, term * D:(term + 1) * D], start=True, stop=True)
                    last.then_inc((y_ready, root_ready)[term], 1)

                def product_round(i, m):
                    for half in range(2):
                        transposes(half, 2 * m + half)
                    for term in range(2):
                        for half in range(2):
                            products(half, term, 2 * m + half)

                if stage == 0:
                    for half in range(2):
                        transposes(half, half)
                    for m in range(NODE_CHUNKS // 2):
                        if m + 1 < NODE_CHUNKS // 2:
                            for half in range(2):
                                transposes(half, 2 * m + 2 + half)
                        for half in range(2):
                            products(half, 0, 2 * m + half)
                            products(half, 1, 2 * m + half)
                else:
                    node_rounds(pe, stage, product_round)

            def edge_products(layer):
                for_nodes = NODE_CHUNKS * (layer + 1)
                pe.wait_ge(y_copied, for_nodes)
                pe.wait_ge(root_stored, for_nodes)
                pe.wait_ge(y_parts_ready, for_nodes)

                def edge_round(i, m):
                    for half in range(2):
                        pe.wait_ge(ea_in[half], 16 * (m + 1))
                        for g in range(CHUNK_GROUPS):
                            n = CHUNK_GROUPS * (2 * m + half) + g
                            slot = half * CHUNK_GROUPS + g
                            before = n - bank_age(slot) + 1
                            if past(before):
                                pe.wait_ge(msg_ready, before)
                            features = ea[:, half, g * P:(g + 1) * P]
                            own = GROUP * D if g not in HOT else HOT[g] * D
                            nc.tensor.matmul(edge_bank(slot)[:, 0:own], features, w_edge_sb[:, layer, 0:own],
                                             start=True, stop=True).then_inc(edge_ready, 1)
                            if g not in HOT:
                                continue
                            q = list(HOT).index(g)
                            hots = HOTS * (2 * m + half) + q + 1
                            if past(hots - 2):
                                pe.wait_ge(hot_copied, hots - 2)
                            nc.tensor.matmul(hot_bank(half, q)[:, 0:D], features, w_edge_sb[:, layer, own:own + D],
                                             start=True, stop=False, skip_group_check=True)
                            pe.wait_ge(onehot_ready, hots)
                            for k in range(NODE_TILES):
                                last = nc.tensor.matmul(
                                    hot_bank(half, q), wide[:, q, k, :],
                                    y_parts[:, k, :, :].rearrange("p s d -> p (s d)"),
                                    start=False, stop=k == NODE_TILES - 1, skip_group_check=True)
                            last.then_inc(hot_ready, 1)

                rounds(pe, layer, edge_round)

            def carry_transposes(layer):
                pe.wait_ge(steps_done, STEPS * (layer + 1))
                if layer:
                    pe.wait_ge(patched_ready, layer)
                nc.tensor.transpose(lastT_ps, ring_step(2 * CHUNK_GROUPS - 1, GROUP - 1),
                                    ident[:, :]).then_inc(lastT_ready, 1)
                pe.wait_ge(carryT_ready, layer + 1)
                nc.tensor.transpose(carry_ps, carryT[:, 0:P], ident[0:D, 0:D]).then_inc(carry_ready, 1)
                pe.wait_ge(patched_ready, layer + 1)

            for layer in range(2):
                node_products(layer)
                edge_products(layer)
                carry_transposes(layer)


def kernel(**inputs):
    import numpy as np
    import concourse.bacc as bacc
    from concourse.bass_utils import run_bass_kernel_spmd

    def get(name):
        return np.asarray(inputs[name])

    x = np.zeros((NODE_ROWS, D), np.float32)
    x[:N_NODES] = get("x")
    src = np.zeros(EDGE_ROWS, np.int32)
    src[:N_EDGES] = get("src")
    dst = np.full(EDGE_ROWS, NODE_ROWS, np.int32)
    dst[:N_EDGES] = get("dst")
    ea = np.zeros((EDGE_ROWS, DE), np.float32)
    ea[:N_EDGES] = get("edge_attr_32")

    before = np.full(EDGE_ROWS, -1, np.int32)
    before.reshape(P, STEPS)[:, 1:] = dst.reshape(P, STEPS)[:, :-1]
    prev_last = np.full((P, 1), -1, np.int32)
    prev_last[1:, 0] = dst.reshape(P, STEPS)[:-1, -1]
    by_chunk = lambda a: a.reshape(P, CHUNKS, CHUNK).transpose(1, 0, 2)
    meta = np.concatenate([by_chunk(src), by_chunk(before)[:, :, :1], by_chunk(dst)], axis=2)
    ea_t = ea.reshape(P, CHUNKS, CHUNK_GROUPS, GROUP, DE).transpose(1, 3, 4, 2, 0)
    dst_rows = dst.reshape(SEARCH, SEARCH)
    hot_steps = [GROUP * g + j for g, j in HOT.items()]
    hot_src = src.reshape(P, CHUNKS, CHUNK)[:, :, hot_steps].transpose(1, 2, 0).reshape(CHUNKS, 1, HOTS * P)
    hot_src = np.concatenate([hot_src, hot_src[:2]])
    ea_t = ea_t.reshape(CHUNKS, GROUP * DE, CHUNK_GROUPS * P)
    ea_t = np.concatenate([ea_t, ea_t[:2]])
    meta = np.concatenate([meta, meta[:2]])

    arrays = {
        "x_rows": x,
        "meta": meta,
        "hot_src": hot_src,
        "ea_t": ea_t,
        "dst_runs": dst.reshape(P, STEPS),
        "prev_last": prev_last,
        "dst_rows": dst_rows,
        "row_last": dst_rows[:, -1].reshape(1, SEARCH),
        "w_node1": np.concatenate([get("L0_gnn_W1_msg"), get("L0_gnn_W1_root")], axis=1),
        "w_node2": np.concatenate([get("L0_gnn_W2_msg"), get("L0_gnn_W2_root")], axis=1),
        "w_edge1": get("L0_gnn_W1_edge"),
        "w_edge2": get("L0_gnn_W2_edge"),
        "bias1": get("L0_gnn_b1").reshape(1, D),
        "bias2": get("L0_gnn_b2").reshape(1, D),
    }
    arrays = {name: np.ascontiguousarray(a) for name, a in arrays.items()}

    nc = bacc.Bacc("TRN2", target_bir_lowering=False, num_devices=1)
    ap = {name: nc.dram_tensor(name, a.shape, mybir.dt.from_np(a.dtype), kind="ExternalInput").ap()
          for name, a in arrays.items()}
    out = nc.dram_tensor("out", (NODE_ROWS, D), mybir.dt.float32, kind="ExternalOutput").ap()
    build(nc, ap["x_rows"], ap["meta"], ap["hot_src"], ap["ea_t"], ap["dst_runs"], ap["prev_last"], ap["dst_rows"],
          ap["row_last"], [ap["w_node1"], ap["w_node2"]], [ap["w_edge1"], ap["w_edge2"]],
          [ap["bias1"], ap["bias2"]], out)
    r = run_bass_kernel_spmd(nc, [arrays], core_ids=[0])
    return r.results[0]["out"][:N_NODES]
```
